# Optimizing a Trainium2 kernel written in Bass

```python
import numpy as np
import jax
import jax.numpy as jnp

def _softmax(x, axis=-1):
    return jax.nn.softmax(x, axis=axis)

def _gelu(x):
    return jax.nn.gelu(x, approximate=True)

def _silu(x):
    return jax.nn.silu(x)

def _sigmoid(x):
    return jax.nn.sigmoid(x)

def _layernorm(x, axis=-1, eps=1e-05):
    m = jnp.mean(x, axis=axis, keepdims=True)
    v = jnp.var(x, axis=axis, keepdims=True)
    return (x - m) / jnp.sqrt(v + eps)

def _scatter_add(tgt, idx, src, axis=0):
    return tgt.at[idx].add(src)

def _segment_sum(src, seg, n):
    return jax.ops.segment_sum(src, seg, n)
kernel_name = 'mk_decoder_preln_d1_seqx_r4_25f238'

def setup_inputs(seed: int=0):
    np.random.seed(seed)
    _w = jnp.asarray

    def _rec_inputs():
        import jax
        import jax.numpy as jnp
        _rk = jax.random.key(seed)
        x = -0.000125 + 0.9999 * jax.random.normal(jax.random.fold_in(_rk, 1), (16, 128, 512), jnp.float32)
        _lenS = 128 - jax.random.randint(jax.random.fold_in(_rk, 7), (16,), 0, max(1, 128 // 4) + 1, jnp.int32)
        _lenS2 = 128 - jax.random.randint(jax.random.fold_in(_rk, 8), (16,), 0, max(1, 128 // 4) + 1, jnp.int32)
        _ctx_2048P = jax.random.normal(jax.random.fold_in(_rk, 11), (16, 16, 512), jnp.float32)
        _ctx_2048c = jax.random.dirichlet(jax.random.fold_in(_rk, 511), 0.3 * jnp.ones((16,), jnp.float32), (16, 128))
        _ctx_2048t = jnp.einsum('bsk,bkd->bsd', _ctx_2048c, _ctx_2048P)
        _ctx_2048t = _ctx_2048t * jax.lax.rsqrt(jnp.mean(jnp.square(_ctx_2048t)) + 1e-12) * 0.953939
        ctx_2048 = -0.000514642 + 1.00011 * (_ctx_2048t + 0.3 * jax.random.normal(jax.random.fold_in(_rk, 611), (16, 128, 512), jnp.float32))
        _validS = jnp.arange(128)[None, :] < _lenS[:, None]
        _validS2 = jnp.arange(128)[None, :] < _lenS2[:, None]
        _causal = jnp.tril(jnp.ones((128, 128), dtype=bool))
        mask_BxS2_bk0 = jnp.logical_not(jnp.broadcast_to(_validS2[:, :], (16, 128)))
        return (x, ctx_2048, mask_BxS2_bk0)
    x, ctx_2048, mask_BxS2_bk0 = _rec_inputs()

    def _L0_attn_setup():
        import jax, jax.numpy as jnp
        import numpy as np
        import math
        B, S, D, H = (4, 512, 512, 16)
        HD = D // H

        def _alibi_slopes(n_heads):
            return jnp.asarray([2.0 ** (-8.0 / n_heads * (h + 1)) for h in range(n_heads)], dtype=jnp.float32)
        key = jax.random.key(seed)
        ks = jax.random.split(key, 10)
        w = lambda k: jax.random.normal(k, (D, D), dtype=jnp.float32) * 0.02
        b = lambda k: jax.random.normal(k, (D,), dtype=jnp.float32) * 0.01
        return {'hidden_states': jax.random.normal(ks[0], (B, S, D), dtype=jnp.float32), 'Wq': w(ks[1]), 'bq': b(ks[2]), 'Wk': w(ks[3]), 'bk': b(ks[4]), 'Wv': w(ks[5]), 'bv': b(ks[6]), 'Wo': w(ks[7]), 'bo': b(ks[8]), 'alibi_slopes': _alibi_slopes(H)}
    _L0_attn_all = _L0_attn_setup()
    _L0_attn_in = {k: v for k, v in _L0_attn_all.items() if k in ('Wq', 'bq', 'Wk', 'bk', 'Wv', 'bv', 'Wo', 'bo', 'alibi_slopes')}
    del _L0_attn_all

    def _L0_xattn_setup():
        import jax, jax.numpy as jnp
        import numpy as np
        key = jax.random.key(seed)
        k1, k2, k3 = jax.random.split(key, 3)
        B, S, D, M = (8, 512, 512, 128)
        hidden_states = jax.random.normal(k1, (B, S, D), dtype=jnp.float32)
        memory_tokens = jax.random.normal(k2, (B, M, D), dtype=jnp.float32)
        memory_mask = jax.random.randint(k3, (B, M), 0, 2).astype(jnp.bool_)
        return {'hidden_states': hidden_states, 'memory_tokens': memory_tokens, 'memory_mask': memory_mask}
    _L0_xattn_all = _L0_xattn_setup()
    _L0_xattn_in = {k: v for k, v in _L0_xattn_all.items() if k in ()}
    del _L0_xattn_all

    def _L0_ffn_setup():
        import jax, jax.numpy as jnp
        import numpy as np
        B, S, H, I = (1, 64, 512, 1536)

        def _quantized_matmul(x, w, scale):
            wq = w.astype(jnp.float8_e4m3fn).astype(x.dtype)
            y = jnp.einsum('bsi,io->bso', x, wq)
            return y * scale
        key = jax.random.key(seed)
        ks = jax.random.split(key, 7)
        return {'x': jax.random.normal(ks[0], (B, S, H), dtype=jnp.float32), 'gate_w': jax.random.normal(ks[1], (H, I), dtype=jnp.float32) * 0.02, 'up_w': jax.random.normal(ks[2], (H, I), dtype=jnp.float32) * 0.02, 'down_w': jax.random.normal(ks[3], (I, H), dtype=jnp.float32) * 0.02, 'gate_scale': jax.random.uniform(ks[4], (I,), dtype=jnp.float32, minval=0.5, maxval=1.5), 'up_scale': jax.random.uniform(ks[5], (I,), dtype=jnp.float32, minval=0.5, maxval=1.5), 'down_scale': jax.random.uniform(ks[6], (H,), dtype=jnp.float32, minval=0.5, maxval=1.5)}
    _L0_ffn_all = _L0_ffn_setup()
    _L0_ffn_in = {k: v for k, v in _L0_ffn_all.items() if k in ('gate_w', 'up_w', 'down_w', 'gate_scale', 'up_scale', 'down_scale')}
    del _L0_ffn_all
    return {'x': x, 'ctx_2048': ctx_2048, 'mask_BxS2_bk0': mask_BxS2_bk0, 'L0_attn_Wq': _L0_attn_in['Wq'], 'L0_attn_bq': _L0_attn_in['bq'], 'L0_attn_Wk': _L0_attn_in['Wk'], 'L0_attn_bk': _L0_attn_in['bk'], 'L0_attn_Wv': _L0_attn_in['Wv'], 'L0_attn_bv': _L0_attn_in['bv'], 'L0_attn_Wo': _L0_attn_in['Wo'], 'L0_attn_bo': _L0_attn_in['bo'], 'L0_attn_alibi_slopes': _L0_attn_in['alibi_slopes'], 'L0_ffn_gate_w': _L0_ffn_in['gate_w'], 'L0_ffn_up_w': _L0_ffn_in['up_w'], 'L0_ffn_down_w': _L0_ffn_in['down_w'], 'L0_ffn_gate_scale': _L0_ffn_in['gate_scale'], 'L0_ffn_up_scale': _L0_ffn_in['up_scale'], 'L0_ffn_down_scale': _L0_ffn_in['down_scale']}

def reference(x, ctx_2048, mask_BxS2_bk0, L0_attn_Wq, L0_attn_bq, L0_attn_Wk, L0_attn_bk, L0_attn_Wv, L0_attn_bv, L0_attn_Wo, L0_attn_bo, L0_attn_alibi_slopes, L0_ffn_gate_w, L0_ffn_up_w, L0_ffn_down_w, L0_ffn_gate_scale, L0_ffn_up_scale, L0_ffn_down_scale):
    import jax
    import jax.numpy as jnp

    def _L0_attn_ref(hidden_states, Wq, bq, Wk, bk, Wv, bv, Wo, bo, alibi_slopes):
        import jax, jax.numpy as jnp
        import numpy as np
        import math
        B, S, D, H = (4, 512, 512, 16)
        HD = D // H

        def _alibi_slopes(n_heads):
            return jnp.asarray([2.0 ** (-8.0 / n_heads * (h + 1)) for h in range(n_heads)], dtype=jnp.float32)
        Bn, t, _ = hidden_states.shape
        split = lambda x: x.reshape(Bn, t, H, HD).transpose(0, 2, 1, 3)
        q = split(hidden_states @ Wq.T + bq)
        k = split(hidden_states @ Wk.T + bk)
        v = split(hidden_states @ Wv.T + bv)
        scores = jnp.einsum('bhsd,bhtd->bhst', q, k)
        pos = jnp.arange(t)
        rel = (pos[None, :] - pos[:, None]).astype(scores.dtype)
        bias = alibi_slopes[:, None, None] * rel
        scores = (scores + bias[None]) / math.sqrt(HD)
        scores = 30.0 * jnp.tanh(scores / 30.0)
        causal = pos[:, None] >= pos[None, :]
        scores = jnp.where(causal[None, None], scores, -jnp.inf)
        probs = jax.nn.softmax(scores, axis=-1)
        ctx = jnp.einsum('bhst,bhtd->bhsd', probs, v)
        ctx = ctx.transpose(0, 2, 1, 3).reshape(Bn, t, D)
        return ctx @ Wo.T + bo

    def _L0_xattn_ref(hidden_states, memory_tokens, memory_mask):
        import jax, jax.numpy as jnp
        import numpy as np
        B, S, D = hidden_states.shape
        scale = 1.0 / jnp.sqrt(jnp.asarray(D, hidden_states.dtype))
        scores = jnp.einsum('bsd,bmd->bsm', hidden_states, memory_tokens) * scale
        neg_inf = jnp.asarray(-1e+30, scores.dtype)
        scores = jnp.where(memory_mask[:, None, :], scores, neg_inf)
        attn = jax.nn.softmax(scores, axis=-1)
        readout = jnp.einsum('bsm,bmd->bsd', attn, memory_tokens)
        valid_b = jnp.any(memory_mask, axis=-1)
        out = jnp.where(valid_b[:, None, None], readout, jnp.zeros_like(readout))
        return out

    def _L0_ffn_ref(x, gate_w, up_w, down_w, gate_scale, up_scale, down_scale):
        import jax, jax.numpy as jnp
        import numpy as np
        B, S, H, I = (1, 64, 512, 1536)

        def _quantized_matmul(x, w, scale):
            wq = w.astype(jnp.float8_e4m3fn).astype(x.dtype)
            y = jnp.einsum('bsi,io->bso', x, wq)
            return y * scale
        gate = jax.nn.silu(_quantized_matmul(x, gate_w, gate_scale))
        up = _quantized_matmul(x, up_w, up_scale)
        fuse = gate * up
        return _quantized_matmul(fuse, down_w, down_scale)
    x = x + _L0_attn_ref(_layernorm(x, axis=-1), L0_attn_Wq, L0_attn_bq, L0_attn_Wk, L0_attn_bk, L0_attn_Wv, L0_attn_bv, L0_attn_Wo, L0_attn_bo, L0_attn_alibi_slopes)
    x = x + _L0_xattn_ref(_layernorm(x, axis=-1), ctx_2048, mask_BxS2_bk0)
    x = x + _L0_ffn_ref(_layernorm(x, axis=-1), L0_ffn_gate_w, L0_ffn_up_w, L0_ffn_down_w, L0_ffn_gate_scale, L0_ffn_up_scale, L0_ffn_down_scale)
    return x

_drawn_inputs = setup_inputs


def setup_inputs(seed=0):
    import zlib

    import numpy as np

    out = dict(_drawn_inputs(seed))
    spreads = {}
    factors = {'L0_attn_Wq': 7.435,
     'L0_attn_bq': 53.141,
     'L0_attn_Wk': 7.128,
     'L0_attn_bk': 64.0,
     'L0_attn_bv': 8.0,
     'L0_attn_bo': 6.472,
     'L0_attn_alibi_slopes': 4.259}
    for name, (base, spread) in spreads.items():
        noise = np.random.default_rng([zlib.crc32(name.encode()), seed]).standard_normal(out[name].shape)
        drawn = base * np.exp(spread * noise) if base else spread * noise
        out[name] = jnp.asarray(drawn.astype(out[name].dtype))
    for name, factor in factors.items():
        out[name] = (out[name] * factor).astype(out[name].dtype)
    return out
```

```python
from contextlib import ExitStack

import concourse.bass as bass
from concourse import mybir

B, S, D, H, F = 16, 128, 512, 16, 1536
HD = D // H
P = 128
KT = D // P
GT = 4
G = B // GT
TG = GT * S
HG = H // 4
FT = F // P
EPS = 1e-5
CAP = 30.0
X_SCALE = float(D) ** -0.5
NEG = 1e30

EXPONENT_BITS = 0x7F800000
MIN_NORMAL = 2.0 ** -6
ROUNDER = 1.5 * 2.0 ** 20
TO_NAN = 3.4028234663852886e38 / 464.0

ALU = mybir.AluOpType
ACT = mybir.ActivationFunctionType
AX = mybir.AxisListType
F32 = mybir.dt.float32
F32R = mybir.dt.float32r
U32 = mybir.dt.uint32
U8 = mybir.dt.uint8


def attention_order(g):
    order = []
    if g < G:
        order += [("T1", i) for i in range(GT)] + [("V", i) for i in range(GT)]
    if g > 0:
        order += [("WO", i) for i in range(GT)]
    if g < G:
        order += [("Q", 0), ("K", 0)]
    for hg in range(HG):
        order += slot_items(g, 2 * hg)
        if g < G and hg + 1 < HG:
            order += [("Q", hg + 1), ("K", hg + 1)]
        order += slot_items(g, 2 * hg + 1)
    return order


def is_now(g, n):
    return isinstance(g, int) and g == n


def slot_items(g, k):
    if is_now(g, 0):
        return []
    return [(n, k - lag) for n, lag in (("RO", 3), ("PT", 2), ("XS", 1), ("T2", 0)) if 0 <= k - lag < GT]


def ffn_order():
    order = []
    for f in range(FT):
        order += [("G", f), ("U", f)]
    order += [("T3", i) for i in range(GT)] + [("D", i) for i in range(GT)]
    return order


FIRST_USES = len(attention_order(0))
LOOP_USES = len(attention_order(1))
FFN_USES = len(ffn_order())
assert FIRST_USES % 2 == 0 and LOOP_USES % 2 == 0 and FFN_USES % 8 == 0


def build(nc, x, memT, mem, mask, wT, bq, bk, bv, bo, slopes, gate_w, up_w, down_w, gate_s, up_s, down_s, out):
    quantized = nc.dram_tensor("quantized", [FT, 3, P, 512], F32).ap()

    with ExitStack() as ctx:
        def sb(name, shape, dt, where=ctx):
            return where.enter_context(nc.sbuf_tensor(name, shape, dt))

        def sem(name):
            return ctx.enter_context(nc.semaphore(name))

        bank = [ctx.enter_context(nc.psum_tensor(f"bank{n}", [P, 512], F32)) for n in range(8)]
        proj_bank, score_bank, ctx_bank, den_bank = bank[0:2], bank[2:6], bank[6], bank[7]

        x_res = sb("x_res", [P, B, D], F32)
        xn = sb("xn", [P, GT, D], F32)
        identity = sb("identity", [P, P], F32)
        bn = sb("bn", [P, GT, 6], F32)
        mv = sb("mv", [P, GT, 2], F32)
        var_eps = sb("var_eps", [P, GT], F32)
        rstd = sb("rstd", [P, GT], F32)
        minus_half = sb("minus_half", [P, GT], F32)
        gate_c = sb("gate_c", [P, FT], F32)
        up_c = sb("up_c", [P, FT], F32)
        half_gate = sb("half_gate", [P, FT], F32)
        fuse_c = sb("fuse_c", [P, FT], F32)
        R_QKV, R_WO, R_XT, R_CT, R_END = 0, 12288, 16384, 20480, 24576
        reduced = sb("reduced", [P, R_END], F32R)
        w_hi = reduced[:, 0:6144].rearrange("p (m k n) -> p m k n", m=3, k=KT)
        w_lo = reduced[:, 6144:12288].rearrange("p (m k n) -> p m k n", m=3, k=KT)
        wo_hi = reduced[:, R_WO:R_WO + 2048].rearrange("p (k n) -> p k n", k=KT)
        wo_lo = reduced[:, R_WO + 2048:R_XT].rearrange("p (k n) -> p k n", k=KT)
        xT_hi = reduced[:, R_XT:R_XT + 2048].rearrange("p (k n) -> p k n", k=KT)
        xT_lo = reduced[:, R_XT + 2048:R_CT].rearrange("p (k n) -> p k n", k=KT)
        cT_hi = reduced[:, R_CT:R_CT + 2048].rearrange("p (k n) -> p k n", k=KT)
        cT_lo = reduced[:, R_CT + 2048:R_END].rearrange("p (k n) -> p k n", k=KT)
        gu_w = reduced[:, 0:12288].rearrange("p (f w k n) -> p f w k n", f=FT, w=2, k=KT)
        down_q = reduced[:, R_WO:R_WO + 6144].rearrange("p (f n) -> p f n", f=FT)
        x3_hi, x3_lo = cT_hi, cT_lo

        att = ExitStack()
        with att:
            qbd = sb("qbd", [P, 4, TG], F32, att)
            kT = sb("kT", [P, TG], F32, att)
            v = sb("v", [P, GT, D], F32, att)
            probs = sb("probs", [P, GT, 4, S], F32, att)
            recip = sb("recip", [P, TG], F32, att)
            ctxT = sb("ctxT", [P, TG], F32, att)
            alibi = sb("alibi", [P, H, S], F32, att)
            x2T = sb("x2T", [P, KT, S], F32, att)
            memT_sb = sb("memT_sb", [P, 2, KT, S], F32, att)
            mem_sb = sb("mem_sb", [P, 2, D], F32, att)
            q_w = sb("q_w", [P, 2, 512], F32, att)
            q_m = sb("q_m", [P, 512], F32, att)
            q_z = sb("q_z", [P, 512], F32, att)
            mask_u8 = sb("mask_u8", [P, B, S], U8, att)
            mask_mul = sb("mask_mul", [P, GT, S], F32, att)
            mask_add = sb("mask_add", [P, GT, S], F32, att)
            valid = sb("valid", [P, GT], F32, att)
            x_sc = sb("x_sc", [P, 2, S], F32, att)
            x_p = sb("x_p", [P, 2, S], F32, att)
            x_pT = sb("x_pT", [P, 2, S], F32, att)
            x_bias = sb("x_bias", [P, 2], F32, att)
            x_den = sb("x_den", [P, 2], F32, att)
            x_rec = sb("x_rec", [P, 2], F32, att)
            x_w = sb("x_w", [P, 2], F32, att)
            bq_c = sb("bq_c", [P, HG], F32, att)
            bk_c = sb("bk_c", [P, HG], F32, att)
            bv_b = sb("bv_b", [P, D], F32, att)
            bo_b = sb("bo_b", [P, D], F32, att)
            slope_b = sb("slope_b", [P, H], F32, att)
            rel = sb("rel", [P, S], F32, att)
            ones = sb("ones", [P, HD], F32, att)
        ffn = ExitStack()
        with ffn:
            f_hi = sb("f_hi", [P, FT, TG], F32R, ffn)
            f_lo = sb("f_lo", [P, FT, TG], F32R, ffn)
            tanh_g = sb("tanh_g", [P, 2, TG], F32, ffn)
            silu2 = sb("silu2", [P, 2, TG], F32, ffn)
            fused = sb("fused", [P, 2, TG], F32, ffn)
            y_sb = sb("y_sb", [P, 2, D], F32, ffn)
            down_c = sb("down_c", [P, D], F32, ffn)

        raw = [x_res[:, GT * (m + 1):GT * (m + 2), :].rearrange("p i n -> p (i n)") for m in range(3)]
        raw += [probs[:].rearrange("p i j s -> p (i j s)")]

        x_first_loaded, x_rest_loaded = sem("x_first_loaded"), sem("x_rest_loaded")
        raw_loaded = [sem(f"raw_loaded{m}") for m in range(4)]
        params_loaded = sem("params_loaded")
        consts_made, identity_made, rel_made = sem("consts_made"), sem("identity_made"), sem("rel_made")
        w_hi_made, w_lo_made = sem("w_hi_made"), sem("w_lo_made")
        qbd_zeroed, alibi_made = sem("qbd_zeroed"), sem("alibi_made")
        fuse_c_made = sem("fuse_c_made")
        bn_done, var_ready, eps_added, rstd_ready, xn_ready = (
            sem("bn_done"), sem("var_ready"), sem("eps_added"), sem("rstd_ready"), sem("xn_ready"))
        proj_filled = [sem(f"proj_filled{n}") for n in range(2)]
        proj_drained = [sem(f"proj_drained{n}") for n in range(2)]
        xT_hi_ready, v_ready, k_ready, q_ready = (
            sem("xT_hi_ready"), sem("v_ready"), sem("k_ready"), sem("q_ready"))
        scores_filled, biased, tanhed, exped, masked = (
            sem("scores_filled"), sem("biased"), sem("tanhed"), sem("exped"), sem("masked"))
        ctx_filled, recip_done, ctx_normed, ctx_hi, ctx_lo = (
            sem("ctx_filled"), sem("recip_done"), sem("ctx_normed"), sem("ctx_hi"), sem("ctx_lo"))
        wo_added, attn_added = sem("wo_added"), sem("attn_added")
        memT_loaded = [sem(f"memT_loaded{n}") for n in range(2)]
        mem_loaded = [sem(f"mem_loaded{n}") for n in range(2)]
        mask_step, mask_ready = sem("mask_step"), sem("mask_ready")
        xs_step, xs_ready, xs_exped, xs_weight, x2_added = (
            sem("xs_step"), sem("xs_ready"), sem("xs_exped"), sem("xs_weight"), sem("x2_added"))
        q_loaded = [sem(f"q_loaded{n}") for n in range(2)]
        q_stored = [sem(f"q_stored{n}") for n in range(2)]
        q_step, q_prepared, q_rounded, q_pool = sem("q_step"), sem("q_prepared"), sem("q_rounded"), sem("q_pool")
        gu_loaded = [sem(f"gu_loaded{n}") for n in range(FT)]
        down_loaded, down_c_loaded = sem("down_loaded"), sem("down_c_loaded")
        filled = [sem(f"filled{n}") for n in range(8)]
        drained = [sem(f"drained{n}") for n in range(8)]
        x3_hi_ready, tanh_ready, f_hi_ready, f_lo_ready = (
            sem("x3_hi_ready"), sem("tanh_ready"), sem("f_hi_ready"), sem("f_lo_ready"))
        y_ready = sem("y_ready")
        y_stored = [sem(f"y_stored{n}") for n in range(2)]

        def proj_use(item, g):
            shape = 0 if is_now(g, 0) else (G if is_now(g, G) else 1)
            at = attention_order(shape).index(item)
            if shape == 0:
                return at % 2, at // 2
            return at % 2, FIRST_USES // 2 + at // 2 + (g - 1) * (LOOP_USES // 2)

        def ffn_use(item, g):
            at = ffn_order().index(item)
            return at % 8, at // 8 + g * (FFN_USES // 8)

        def t3_use(g, i):
            b_, u = ffn_use(("T3", i), 0)
            return b_, u + 1 + (g - 1) * (FFN_USES // 8)

        def gu_use(item, g):
            b_, u = ffn_use(item, g)
            return b_, u + (1 if b_ < GT else 0)

        def wait_apart(e, semaphore, value):
            e.wait_ge(semaphore, value)
            if not isinstance(value, int):
                e.nop(nofuse=True)

        def wait_proj(e, item, g):
            b, n = proj_use(item, g)
            e.wait_ge(proj_filled[b], n + 1)
            return proj_bank[b]

        def proj_sem(item, g):
            return proj_drained[proj_use(item, g)[0]]

        block = ctx.enter_context(nc.Block())

        @block.sync
        def _(sp):
            x_t = x.rearrange("b s d -> s b d")
            sp.dma_start(x_res[:, 0:GT, :], x_t[:, 0:GT, :]).then_inc(x_first_loaded, 16)
            for m in (2, 0, 1, 3):
                sp.dma_start(raw[m].rearrange("p (k n) -> p k n", k=KT),
                             wT[m].rearrange("(k p) n -> p k n", p=P)).then_inc(raw_loaded[m], 16)
            for dst, src in ((bq_c[:], bq), (bk_c[:], bk), (gate_c[:], gate_s), (up_c[:], up_s),
                             (slope_b[:], slopes.partition_broadcast(P)), (bv_b[:], bv.partition_broadcast(P)),
                             (bo_b[:], bo.partition_broadcast(P)),
                             (mask_u8[:].rearrange("p b s -> p (b s)"), mask.partition_broadcast(P))):
                sp.dma_start(dst, src).then_inc(params_loaded, 16)
            sp.wait_ge(w_lo_made, 3)
            sp.dma_start(x_res[:, GT:B, :], x_t[:, GT:B, :]).then_inc(x_rest_loaded, 16)

            def quantize_slab(g, hg, c):
                n = 3 * hg + c
                f = (g - 1) * HG + hg
                src = (gate_w, up_w)[c].rearrange("(k p) (f m) -> f p k m", p=P, m=P) if c < 2 else \
                    down_w.rearrange("(f p) n -> f p n", p=P)
                dst = q_w[:, n % 2, :]
                if n >= 2:
                    wait_apart(sp, q_stored[n % 2], 16 * (n // 2) + (g - 1) * 96)
                if c < 2:
                    dst = dst.rearrange("p (k m) -> p k m", k=KT)
                    sp.dma_start(dst, src[bass.ds(f, 1)].rearrange("a p k m -> p (a k) m")).then_inc(q_loaded[n % 2], 16)
                else:
                    sp.dma_start(dst, src[bass.ds(f, 1)].rearrange("a p n -> p (a n)")).then_inc(q_loaded[n % 2], 16)

            def store_slab(g, hg, c):
                n = 3 * hg + c
                f = (g - 1) * HG + hg
                wait_apart(sp, q_rounded, n + 1 + (g - 1) * 12)
                sp.dma_start(quantized[bass.ds(f, 1), c].rearrange("a p n -> p (a n)"), q_w[:, n % 2, :])\
                    .then_inc(q_stored[n % 2], 16)

            def load_memT(g, i):
                b = (g - 1) * GT + i
                n = i % 2
                if i >= 2:
                    bk_, u = proj_use(("XS", i - 2), g)
                    wait_apart(sp, proj_filled[bk_], u + 1)
                sp.dma_start(memT_sb[:, n], memT[bass.ds(b, 1)].rearrange("a (k p) m -> p (a k) m", p=P))\
                    .then_inc(memT_loaded[n], 16)

            def load_mem(g, i):
                b = (g - 1) * GT + i
                n = i % 2
                if i >= 2:
                    bk_, u = proj_use(("RO", i - 2), g)
                    wait_apart(sp, proj_filled[bk_], u + 1)
                sp.dma_start(mem_sb[:, n], mem[bass.ds(b, 1)].rearrange("a m d -> m (a d)"))\
                    .then_inc(mem_loaded[n], 16)

            def iteration(g):
                between = {2: [(load_memT, 2)], 4: [(load_memT, 3), (load_mem, 2)], 7: [(load_mem, 3)]}
                slabs = [(hg, c) for hg in range(HG) for c in range(3)]
                for i in range(2):
                    load_memT(g, i)
                    load_mem(g, i)
                for n, (hg, c) in enumerate(slabs):
                    if n >= 2:
                        store_slab(g, *slabs[n - 2])
                    quantize_slab(g, hg, c)
                    for load, i in between.get(n, []):
                        load(g, i)
                store_slab(g, *slabs[-2])
                store_slab(g, *slabs[-1])
                for i in (2, 3):
                    bk_, u = proj_use(("RO", i), g)
                    wait_apart(sp, proj_filled[bk_], u + 1)
                for n in range(2):
                    wait_apart(sp, q_stored[n], 96 + (g - 1) * 96)

            with sp.Fori(1, G) as g:
                iteration(g)
            for i in range(2):
                load_memT(G, i)
                load_mem(G, i)
            b_, u = proj_use(("K", HG - 1), G - 1)
            sp.wait_ge(proj_filled[b_], u + 1)
            for f in range(FT):
                if f == GT:
                    load_memT(G, 2)
                    load_memT(G, 3)
                    load_mem(G, 2)
                    load_mem(G, 3)
                sp.dma_start(gu_w[:, f].rearrange("p w k n -> p w (k n)").bitcast(F32),
                             quantized[f, 0:2].rearrange("w p n -> p w n")).then_inc(gu_loaded[f], 16)
            b_, u = proj_use(("WO", GT - 1), G)
            sp.wait_ge(proj_filled[b_], u + 1)
            sp.dma_start(down_q.bitcast(F32), quantized[:, 2].rearrange("f p n -> p f n")).then_inc(down_loaded, 16)

            for i in (2, 3):
                b_, u = proj_use(("RO", i), G)
                sp.wait_ge(proj_drained[b_], 2 * (u + 1))
            sp.dma_start(down_c[:], down_s.partition_broadcast(P)).then_inc(down_c_loaded, 16)

            def store_out(g):
                for i in range(GT):
                    wait_apart(sp, y_ready, i + 1 + g * GT)
                    sp.dma_start(out[bass.ds(g * GT + i, 1)].rearrange("a s d -> s (a d)"), y_sb[:, i % 2, :])\
                        .then_inc(y_stored[i % 2], 16)

            with sp.Fori(0, G) as g:
                store_out(g)
            sp.wait_ge(y_stored[0], 16 * B // 2)
            sp.wait_ge(y_stored[1], 16 * B // 2)

        @block.gpsimd
        def _(pool):
            pool.memset(identity[:], 0.0).then_inc(consts_made, 1)
            pool.memset(ones[:], 1.0).then_inc(consts_made, 1)
            pool.memset(minus_half[:], -0.5).then_inc(consts_made, 1)
            pool.iota(rel[:], pattern=[[-1, S]], base=0, channel_multiplier=1,
                      allow_small_or_imprecise_dtypes=True).then_inc(rel_made, 1)
            pool.wait_ge(consts_made, 3)
            pool.affine_select(out=identity[:], in_=identity[:], compare_op=ALU.not_equal, fill=1.0,
                               base=0, pattern=[[-1, P]], channel_multiplier=1).then_inc(identity_made, 1)

            def norm_scale(n):
                wait_apart(pool, var_ready, n * GT + GT)
                pool.tensor_scalar(var_eps[:], mv[:, :, 1], EPS, 1.0, ALU.add, ALU.mult).then_inc(eps_added, 1)
                pool.wait_ge(eps_added, n + 1)
                pool.tensor_tensor(rstd[:], var_eps[:], minus_half[:], ALU.pow).then_inc(rstd_ready, 1)

            def low_part(g, hg):
                m = g * HG + hg
                pool.wait_ge(ctx_hi, m + 1)
                pool.tensor_tensor(cT_lo[:, hg, :], ctxT[:], cT_hi[:, hg, :].bitcast(F32), ALU.subtract)\
                    .then_inc(ctx_lo, 1)

            def causal(g, hg):
                for i in range(GT):
                    wait_apart(pool, exped, (g * HG + hg) * GT + i + 1)
                    pool.affine_select(out=probs[:, i], in_=probs[:, i], compare_op=ALU.is_ge, fill=0.0,
                                       base=0, pattern=[[0, 4], [1, S]], channel_multiplier=-1).then_inc(masked, 1)

            def round_slab(g, n):
                w = q_w[:, n % 2, :]
                at = (g - 1) * 12 + n
                pool.wait_ge(q_prepared, at + 1)
                pool.tensor_tensor(w, w, q_z[:], ALU.add).then_inc(q_pool, 1)
                pool.wait_ge(q_pool, 2 * at + 1)
                pool.tensor_tensor(w, w, q_m[:], ALU.add).then_inc(q_pool, 1)
                pool.wait_ge(q_pool, 2 * at + 2)
                pool.tensor_tensor(w, w, q_m[:], ALU.subtract).then_inc(q_rounded, 1)

            norm_scale(0)
            for hg in range(HG):
                causal(0, hg)
                if hg + 1 < HG:
                    low_part(0, hg)
            with pool.Fori(1, G) as g:
                norm_scale(2 * g - 1)
                low_part(g - 1, HG - 1)
                norm_scale(2 * g)
                for hg in range(HG):
                    causal(g, hg)
                    for c in range(3):
                        round_slab(g, 3 * hg + c)
                    if hg + 1 < HG:
                        low_part(g, hg)
            low_part(G - 1, HG - 1)
            norm_scale(2 * G - 1)
            norm_scale(2 * G)

            def ffn_lows(g):
                for f in range(FT):
                    pool.wait_ge(f_hi_ready, g * FT + f + 1)
                    pool.tensor_tensor(f_lo[:, f, :], fused[:, f % 2, :], f_hi[:, f, :].bitcast(F32),
                                       ALU.subtract).then_inc(f_lo_ready, 1)

            with pool.Fori(0, G - 1) as g:
                norm_scale(g + 2 * G + 1)
                ffn_lows(g)
            ffn_lows(G - 1)

        @block.scalar
        def _(act):
            for n, m in enumerate((2, 0, 1, 3)):
                act.wait_ge(raw_loaded[m], 16)
                dst = w_hi[:, m] if m < 3 else wo_hi
                act.activation(dst.rearrange("p k n -> p (k n)"), raw[m], ACT.Copy).then_inc(w_hi_made, 1)

            def x_high(g):
                for i in range(GT):
                    src = wait_proj(act, ("T1", i), g)
                    act.activation(xT_hi[:, :, i * S:(i + 1) * S], src[:].rearrange("p (k s) -> p k s", k=KT),
                                   ACT.Copy).then_inc(xT_hi_ready, 1)

            def q_out(g, hg):
                src = wait_proj(act, ("Q", hg), g)
                if is_now(g, 0) and hg == 0:
                    act.wait_ge(qbd_zeroed, 1)
                    act.wait_ge(params_loaded, 16 * 8)
                for j in range(4):
                    rows = slice(HD * j, HD * (j + 1))
                    ins = act.activation(qbd[rows, j, :], src[rows, :], ACT.Identity, bias=bq_c[rows, hg:hg + 1])
                ins.then_inc(proj_sem(("Q", hg), g), 2)

            def softmax_terms(g, hg):
                def tanh(i):
                    act.wait_ge(biased, (g * HG + hg) * GT + i + 1)
                    act.activation(probs[:, i], probs[:, i], ACT.Tanh, scale=1.0 / (float(HD) ** 0.5 * CAP))\
                        .then_inc(tanhed, 1)

                def exp(i):
                    act.wait_ge(tanhed, (g * HG + hg) * GT + i + 1)
                    act.activation(probs[:, i], probs[:, i], ACT.Exp, scale=CAP).then_inc(exped, 1)

                tanh(0)
                for i in range(1, GT):
                    tanh(i)
                    exp(i - 1)
                exp(GT - 1)

            def context_high(g, hg):
                act.wait_ge(ctx_normed, g * HG + hg + 1)
                act.activation(cT_hi[:, hg, :], ctxT[:], ACT.Copy).then_inc(ctx_hi, 1)

            def slot(g, k):
                for name, i in slot_items(g, k):
                    n = i % 2
                    at = (g - 1) * GT + i
                    if name == "PT":
                        src = wait_proj(act, ("PT", i), g)
                        act.activation(x_pT[:, n, :], src[:, 0:S], ACT.Copy).then_inc(proj_sem(("PT", i), g), 2)
                    if name == "XS":
                        act.wait_ge(xs_ready, at + 1)
                        act.activation(x_p[:, n, :], x_sc[:, n, :], ACT.Exp, bias=x_bias[:, n:n + 1],
                                       accum_out=x_den[:, n:n + 1]).then_inc(xs_exped, 1)
                    if name == "T2":
                        src = wait_proj(act, ("T2", i), g)
                        act.activation(x2T[:].rearrange("p k s -> p (k s)"), src[:], ACT.Copy)\
                            .then_inc(proj_sem(("T2", i), g), 2)

            def heads(g):
                q_out(g, 0)
                for hg in range(HG):
                    softmax_terms(g, hg)
                    slot(g, 2 * hg)
                    if hg + 1 < HG:
                        q_out(g, hg + 1)
                    slot(g, 2 * hg + 1)
                    if hg + 1 < HG:
                        context_high(g, hg)

            x_high(0)
            heads(0)
            with act.Fori(1, G) as g:
                context_high(g - 1, HG - 1)
                x_high(g)
                heads(g)
            context_high(G - 1, HG - 1)
            for k in range(2 * HG):
                slot(G, k)

            def x3_high(g):
                for i in range(GT):
                    bk_, u = t3_use(g, i)
                    act.wait_ge(filled[bk_], u + 1)
                    act.activation(x3_hi[:, :, i * S:(i + 1) * S], bank[bk_][:].rearrange("p (k s) -> p k s", k=KT),
                                   ACT.Copy).then_inc(x3_hi_ready, 1)

            def high(g, f):
                bk_, u = gu_use(("U", f), g)
                act.wait_ge(drained[bk_], 2 * (u + 1))
                act.activation(f_hi[:, f, :], fused[:, f % 2, :], ACT.Copy).then_inc(f_hi_ready, 1)

            def gates(g):
                for f in range(FT):
                    bk_, u = gu_use(("G", f), g)
                    act.wait_ge(filled[bk_], u + 1)
                    act.activation(tanh_g[:, f % 2, :], bank[bk_][:], ACT.Tanh, scale=half_gate[:, f:f + 1])\
                        .then_inc(tanh_ready, 1)
                    if f >= 1:
                        high(g, f - 1)
                high(g, FT - 1)

            x3_high(0)
            act.wait_ge(fuse_c_made, 3)
            with act.Fori(0, G - 1) as g:
                gates(g)
                x3_high(g + 1)
            gates(G - 1)

        @block.vector
        def _(dve):
            def norm(n, tile, wait_tile):
                for i in range(GT):
                    wait_tile(i)
                    dve.bn_stats(bn[:, i, :], tile(i)).then_inc(bn_done, 1)
                for i in range(GT):
                    wait_apart(dve, bn_done, n * GT + i + 1)
                    dve.bn_aggr(mv[:, i, :], bn[:, i, :]).then_inc(var_ready, 1)
                dve.wait_ge(rstd_ready, n + 1)
                for i in range(GT):
                    dve.tensor_scalar(xn[:, i, :], tile(i), mv[:, i, 0:1], rstd[:, i:i + 1], ALU.subtract,
                                      ALU.mult).then_inc(xn_ready, 1)

            def token_tile(g, i):
                if isinstance(g, int):
                    return x_res[:, g * GT + i, :]
                return x_res[:, bass.ds(g * GT + i, 1), :].rearrange("p a n -> p (a n)")

            def x_low(g):
                for i in range(GT):
                    b_, u = proj_use(("T1", i), g)
                    dve.wait_ge(xT_hi_ready, g * GT + i + 1)
                    dve.tensor_tensor(xT_lo[:, :, i * S:(i + 1) * S], proj_bank[b_][:].rearrange("p (k s) -> p k s", k=KT),
                                      xT_hi[:, :, i * S:(i + 1) * S].bitcast(F32), ALU.subtract)\
                        .then_inc(proj_drained[b_], 2)

            def v_out(g):
                for i in range(GT):
                    src = wait_proj(dve, ("V", i), g)
                    dve.tensor_tensor(v[:, i, :], src[:], bv_b[:], ALU.add).then_inc(proj_sem(("V", i), g), 2)

            def wo_out(g):
                for i in range(GT):
                    src = wait_proj(dve, ("WO", i), g)
                    t = token_tile(g - 1, i)
                    dve.tensor_tensor(t, src[:], t, ALU.add).then_inc(proj_sem(("WO", i), g), 2)
                    b_, u = proj_use(("WO", i), g)
                    dve.wait_ge(proj_drained[b_], 2 * (u + 1))
                    dve.tensor_tensor(t, t, bo_b[:], ALU.add).then_inc(attn_added, 1)

            def k_out(g, hg):
                src = wait_proj(dve, ("K", hg), g)
                dve.tensor_scalar(kT[:], src[:], bk_c[:, hg:hg + 1], None, ALU.add).then_inc(proj_sem(("K", hg), g), 2)

            def alibi_add(g, hg):
                m = g * HG + hg
                for i in range(GT):
                    dve.wait_ge(scores_filled, m * GT + i + 1)
                    dve.tensor_tensor(probs[:, i].rearrange("p j s -> p (j s)"), score_bank[i][:],
                                      alibi[:, 4 * hg:4 * hg + 4].rearrange("p j s -> p (j s)"), ALU.add)\
                        .then_inc(biased, 1)

            def normalize_context(g, hg):
                m = g * HG + hg
                dve.wait_ge(ctx_filled, m + 1)
                dve.reciprocal(recip[:], den_bank[:]).then_inc(recip_done, 1)
                dve.wait_ge(recip_done, m + 1)
                if not (is_now(g, 0) and hg == 0):
                    dve.wait_ge(ctx_lo, m)
                dve.tensor_tensor(ctxT[:], ctx_bank[:], recip[:], ALU.mult).then_inc(ctx_normed, 1)

            def masks(g):
                at = g - 1
                dve.tensor_copy(mask_mul[:], mask_u8[:, bass.ds(at * GT, GT), :]).then_inc(mask_step, 1)
                dve.wait_ge(mask_step, 1 + at)
                dve.tensor_scalar(mask_add[:], mask_mul[:], -1.0, NEG, ALU.add, ALU.mult).then_inc(mask_ready, 1)
                dve.tensor_reduce(valid[:], mask_mul[:], AX.X, ALU.max).then_inc(mask_ready, 1)
                dve.wait_ge(mask_ready, 2 + 2 * at)

            def slot(g, k):
                for name, i in slot_items(g, k):
                    n = i % 2
                    at = (g - 1) * GT + i
                    if name == "XS":
                        src = wait_proj(dve, ("XS", i), g)
                        dve.scalar_tensor_tensor(x_sc[:, n, :], src[:, 0:S], X_SCALE, mask_mul[:, i, :], ALU.mult,
                                                 ALU.mult)\
                            .then_inc(proj_sem(("XS", i), g), 2)
                        b_, u = proj_use(("XS", i), g)
                        dve.wait_ge(proj_drained[b_], 2 * (u + 1))
                        dve.tensor_tensor(x_sc[:, n, :], x_sc[:, n, :], mask_add[:, i, :], ALU.add).then_inc(xs_step, 1)
                        dve.wait_ge(xs_step, at + 1)
                        dve.tensor_reduce(x_bias[:, n:n + 1], x_sc[:, n, :], AX.X, ALU.max, negate=True)\
                            .then_inc(xs_ready, 1)
                    if name == "RO":
                        dve.wait_ge(xs_exped, at + 1)
                        dve.reciprocal(x_rec[:, n:n + 1], x_den[:, n:n + 1]).then_inc(xs_weight, 1)
                        dve.wait_ge(xs_weight, 2 * at + 1)
                        dve.tensor_tensor(x_w[:, n:n + 1], x_rec[:, n:n + 1], valid[:, i:i + 1], ALU.mult)\
                            .then_inc(xs_weight, 1)
                        dve.wait_ge(xs_weight, 2 * at + 2)
                        src = wait_proj(dve, ("RO", i), g)
                        t = token_tile(g - 1, i)
                        dve.scalar_tensor_tensor(t, src[:], x_w[:, n:n + 1], t, ALU.mult, ALU.add)\
                            .then_inc(proj_sem(("RO", i), g), 2)

            def prepare_slab(g, n):
                at = (g - 1) * 12 + n
                w = q_w[:, n % 2, :]
                dve.wait_ge(q_loaded[n % 2], 16 * (n // 2 + 1) + (g - 1) * 96)
                if n > 0:
                    dve.wait_ge(q_rounded, at)
                dve.tensor_scalar(q_m[:].bitcast(U32), w.bitcast(U32), EXPONENT_BITS, None, ALU.bitwise_and)\
                    .then_inc(q_step, 1)
                dve.tensor_scalar(q_z[:], w, TO_NAN, 0.0, ALU.mult, ALU.mult).then_inc(q_step, 1)
                dve.wait_ge(q_step, 2 * at + 2)
                dve.tensor_scalar(q_m[:], q_m[:], MIN_NORMAL, ROUNDER, ALU.max, ALU.mult).then_inc(q_prepared, 1)

            def heads(g):
                k_out(g, 0)
                for hg in range(HG):
                    alibi_add(g, hg)
                    slot(g, 2 * hg)
                    if not is_now(g, 0):
                        prepare_slab(g, 3 * hg)
                        prepare_slab(g, 3 * hg + 1)
                    if hg + 1 < HG:
                        k_out(g, hg + 1)
                    slot(g, 2 * hg + 1)
                    if not is_now(g, 0):
                        prepare_slab(g, 3 * hg + 2)
                    if hg + 1 < HG:
                        normalize_context(g, hg)

            def first_norm_wait(i):
                dve.wait_ge(x_first_loaded, 16)

            def no_wait(i):
                pass

            norm(0, lambda i: token_tile(0, i), first_norm_wait)
            for n, m in enumerate((2, 0, 1, 3)):
                if n == 3:
                    v_out(0)
                dve.wait_ge(w_hi_made, n + 1)
                hi, lo = (w_hi[:, m], w_lo[:, m]) if m < 3 else (wo_hi, wo_lo)
                dve.tensor_tensor(lo.rearrange("p k n -> p (k n)"), raw[m],
                                  hi.rearrange("p k n -> p (k n)").bitcast(F32), ALU.subtract)\
                    .then_inc(w_lo_made, 1)
                if n == 0:
                    x_low(0)
                    dve.wait_ge(params_loaded, 16 * 8)
            dve.memset(qbd[:], 0.0).then_inc(qbd_zeroed, 1)
            dve.wait_ge(rel_made, 1)
            for h in range(H):
                ins = dve.tensor_scalar(alibi[:, h, :], rel[:], slope_b[:, h:h + 1], None, ALU.mult)
            ins.then_inc(alibi_made, 1)
            dve.tensor_scalar(half_gate[:], gate_c[:], 0.5, None, ALU.mult).then_inc(fuse_c_made, 1)
            dve.tensor_tensor(fuse_c[:], gate_c[:], up_c[:], ALU.mult).then_inc(fuse_c_made, 1)
            dve.wait_ge(fuse_c_made, 2)
            dve.tensor_scalar(fuse_c[:], fuse_c[:], 0.5, None, ALU.mult).then_inc(fuse_c_made, 1)
            dve.wait_ge(alibi_made, 1)
            heads(0)
            dve.wait_ge(x_rest_loaded, 16)
            with dve.Fori(1, G) as g:
                norm(2 * g - 1, lambda i: token_tile(g, i), no_wait)
                normalize_context(g - 1, HG - 1)
                x_low(g)
                v_out(g)
                wo_out(g)
                masks(g)
                norm(2 * g, lambda i: token_tile(g - 1, i), lambda i: wait_apart(dve, attn_added, (g - 1) * GT + i + 1))
                heads(g)
            normalize_context(G - 1, HG - 1)
            wo_out(G)
            masks(G)
            norm(2 * G - 1, lambda i: token_tile(G - 1, i), lambda i: dve.wait_ge(attn_added, (G - 1) * GT + i + 1))
            for k in range(2 * HG):
                slot(G, k)

            def x3_low(g):
                for i in range(GT):
                    bk_, u = t3_use(g, i)
                    dve.wait_ge(x3_hi_ready, g * GT + i + 1)
                    dve.tensor_tensor(x3_lo[:, :, i * S:(i + 1) * S], bank[bk_][:].rearrange("p (k s) -> p k s", k=KT),
                                      x3_hi[:, :, i * S:(i + 1) * S].bitcast(F32), ALU.subtract)\
                        .then_inc(drained[bk_], 2)

            def fuse(g):
                for f in range(FT):
                    at = g * FT + f
                    bg, ug = gu_use(("G", f), g)
                    bu, uu = gu_use(("U", f), g)
                    dve.wait_ge(tanh_ready, at + 1)
                    dve.scalar_tensor_tensor(silu2[:, f % 2, :], tanh_g[:, f % 2, :], 1.0, bank[bg][:], ALU.add, ALU.mult)\
                        .then_inc(drained[bg], 2)
                    dve.wait_ge(drained[bg], 2 * (ug + 1))
                    dve.wait_ge(filled[bu], uu + 1)
                    if f >= 2:
                        dve.wait_ge(f_lo_ready, at - 1)
                    dve.scalar_tensor_tensor(fused[:, f % 2, :], bank[bu][:], fuse_c[:, f:f + 1], silu2[:, f % 2, :],
                                             ALU.mult, ALU.mult).then_inc(drained[bu], 2)

            def y_out(g):
                dve.wait_ge(down_c_loaded, 16)
                for i in range(GT):
                    bk_, u = gu_use(("D", i), g)
                    at = g * GT + i
                    dve.wait_ge(filled[bk_], u + 1)
                    if i >= 2:
                        dve.wait_ge(y_stored[i % 2], 16 * (i // 2) + g * 32)
                    elif not is_now(g, 0):
                        dve.wait_ge(y_stored[i % 2], g * 32)
                    dve.tensor_tensor(y_sb[:, i % 2, :], bank[bk_][:], down_c[:], ALU.mult).then_inc(drained[bk_], 2)
                    dve.wait_ge(drained[bk_], 2 * (u + 1))
                    dve.tensor_tensor(y_sb[:, i % 2, :], y_sb[:, i % 2, :], token_tile(g, i), ALU.add)\
                        .then_inc(y_ready, 1)

            norm(2 * G, lambda i: token_tile(0, i), no_wait)
            x3_low(0)
            with dve.Fori(0, G - 1) as g:
                norm(g + 2 * G + 1, lambda i: token_tile(g + 1, i), no_wait)
                fuse(g)
                x3_low(g + 1)
                y_out(g)
            fuse(G - 1)
            y_out(G - 1)

        @block.tensor
        def _(pe):
            def take(item, g):
                b_, u = proj_use(item, g)
                if not (is_now(g, 0) and u == 0):
                    pe.wait_ge(proj_drained[b_], 2 * u)
                return proj_bank[b_], proj_filled[b_]

            def transposes(dst, n, i):
                pe.wait_ge(xn_ready, n * GT + i + 1)
                for k in range(KT):
                    ins = pe.transpose(dst[:, k * S:(k + 1) * S], xn[:, i, k * P:(k + 1) * P], identity[:])
                return ins

            def t1(g, n):
                for i in range(GT):
                    dst, done = take(("T1", i), g)
                    transposes(dst, n, i).then_inc(done, 1)

            def products(dst, pairs):
                for n, (stationary, moving) in enumerate(pairs):
                    ins = pe.matmul(dst, stationary, moving, start=(n == 0), stop=(n == len(pairs) - 1))
                return ins

            def v_proj(g):
                for i in range(GT):
                    dst, done = take(("V", i), g)
                    t = slice(i * S, (i + 1) * S)
                    pe.wait_ge(proj_drained[proj_use(("T1", i), g)[0]], 2 * (proj_use(("T1", i), g)[1] + 1))
                    products(dst[:], [p for k in range(KT) for p in (
                        (xT_hi[:, k, t], w_hi[:, 2, k]), (xT_hi[:, k, t], w_lo[:, 2, k]),
                        (xT_lo[:, k, t], w_hi[:, 2, k]))]).then_inc(done, 1)

            def wo_proj(g):
                pe.wait_ge(ctx_lo, g * HG)
                for i in range(GT):
                    dst, done = take(("WO", i), g)
                    t = slice(i * S, (i + 1) * S)
                    products(dst[:], [p for k in range(KT) for p in (
                        (cT_hi[:, k, t], wo_hi[:, k]), (cT_hi[:, k, t], wo_lo[:, k]),
                        (cT_lo[:, k, t], wo_hi[:, k]))]).then_inc(done, 1)

            def qk_proj(g, hg):
                for m, name in ((0, "Q"), (1, "K")):
                    dst, done = take((name, hg), g)
                    n = slice(hg * P, (hg + 1) * P)
                    products(dst[:], [p for k in range(KT) for p in (
                        (w_hi[:, m, k, n], xT_hi[:, k]), (w_hi[:, m, k, n], xT_lo[:, k]),
                        (w_lo[:, m, k, n], xT_hi[:, k]))]).then_inc(done, 1)

            def scores(g, hg):
                m = g * HG + hg
                for name in ("Q", "K"):
                    b_, u = proj_use((name, hg), g)
                    pe.wait_ge(proj_drained[b_], 2 * (u + 1))
                for i in range(GT):
                    t = slice(i * S, (i + 1) * S)
                    if not (is_now(g, 0) and hg == 0):
                        pe.wait_ge(biased, m * GT - GT + i + 1)
                    pe.matmul(score_bank[i][:], kT[:, t], qbd[:, :, t], start=True, stop=True)\
                        .then_inc(scores_filled, 1)

            def context(g, hg):
                m = g * HG + hg
                if not (is_now(g, 0) and hg == 0):
                    pe.wait_ge(ctx_normed, m)
                if hg == 0:
                    b_, u = proj_use(("V", GT - 1), g)
                    pe.wait_ge(proj_drained[b_], 2 * (u + 1))
                    b_, u = proj_use(("V", GT - 2), g)
                    pe.wait_ge(proj_drained[b_], 2 * (u + 1))
                for i in range(GT):
                    t = slice(i * S, (i + 1) * S)
                    pe.wait_ge(masked, m * GT + i + 1)
                    for j in range(4):
                        rows = slice(HD * j, HD * (j + 1))
                        col = hg * P + HD * j
                        pe.matmul(ctx_bank[rows, t], v[:, i, col:col + HD], probs[:, i, j, :], start=True, stop=True)
                    for j in range(4):
                        rows = slice(HD * j, HD * (j + 1))
                        ins = pe.matmul(den_bank[rows, t], ones[:], probs[:, i, j, :], start=True, stop=True)
                ins.then_inc(ctx_filled, 1)

            def slot(g, k):
                for name, i in slot_items(g, k):
                    n = i % 2
                    dst, done = take((name, i), g)
                    if name == "T2":
                        transposes(dst, t2_norm(g), i).then_inc(done, 1)
                    if name == "XS":
                        b_, u = proj_use(("T2", i), g)
                        pe.wait_ge(proj_drained[b_], 2 * (u + 1))
                        pe.wait_ge(memT_loaded[n], 16 * (i // 2 + 1) + (g - 1) * 32)
                        products(dst[:, 0:S], [(x2T[:, k_, :], memT_sb[:, n, k_, :]) for k_ in range(KT)])\
                            .then_inc(done, 1)
                    if name == "PT":
                        pe.wait_ge(xs_exped, (g - 1) * GT + i + 1)
                        pe.transpose(dst[:, 0:S], x_p[:, n, :], identity[:]).then_inc(done, 1)
                    if name == "RO":
                        b_, u = proj_use(("PT", i), g)
                        pe.wait_ge(proj_drained[b_], 2 * (u + 1))
                        pe.wait_ge(mem_loaded[n], 16 * (i // 2 + 1) + (g - 1) * 32)
                        pe.matmul(dst[:], x_pT[:, n, :], mem_sb[:, n, :], start=True, stop=True).then_inc(done, 1)

            def t2_norm(g):
                return 2 * G - 1 if is_now(g, G) else 2 * g

            def heads(g):
                qk_proj(g, 0)
                for hg in range(HG):
                    scores(g, hg)
                    slot(g, 2 * hg)
                    if hg + 1 < HG:
                        qk_proj(g, hg + 1)
                    slot(g, 2 * hg + 1)
                    context(g, hg)

            pe.wait_ge(identity_made, 1)
            t1(0, 0)
            pe.wait_ge(w_lo_made, 1)
            v_proj(0)
            pe.wait_ge(w_lo_made, 3)
            heads(0)
            with pe.Fori(1, G) as g:
                t1(g, 2 * g - 1)
                v_proj(g)
                wo_proj(g)
                heads(g)
            wo_proj(G)
            for k in range(2 * HG):
                slot(G, k)
            for b_ in range(2):
                pe.wait_ge(proj_drained[b_], FIRST_USES + (G - 1) * LOOP_USES + len(attention_order(G)))

            def ffn_take(bk_, u):
                if not (isinstance(u, int) and u == 0):
                    pe.wait_ge(drained[bk_], 2 * u)
                return bank[bk_]

            def t3(g):
                for i in range(GT):
                    bk_, u = t3_use(g, i)
                    dst = ffn_take(bk_, u)
                    transposes(dst, g + 2 * G, i).then_inc(filled[bk_], 1)

            def gate_up(g):
                for i in range(GT):
                    bk_, u = t3_use(g, i)
                    pe.wait_ge(drained[bk_], 2 * (u + 1))
                for f in range(FT):
                    pe.wait_ge(gu_loaded[f], 16)
                    for w, name in ((0, "G"), (1, "U")):
                        bk_, u = gu_use((name, f), g)
                        dst = ffn_take(bk_, u)
                        products(dst[:], [(gu_w[:, f, w, k], x3[:, k]) for k in range(KT) for x3 in (x3_hi, x3_lo)])\
                            .then_inc(filled[bk_], 1)

            def down(g):
                pe.wait_ge(down_loaded, 16)
                for i in range(GT):
                    bk_, u = gu_use(("D", i), g)
                    dst = ffn_take(bk_, u)
                    t = slice(i * S, (i + 1) * S)
                    for f in range(FT):
                        if i == 0:
                            pe.wait_ge(f_lo_ready, g * FT + f + 1)
                        for n, part in enumerate((f_hi, f_lo)):
                            ins = pe.matmul(dst[:], part[:, f, t], down_q[:, f], start=(f + n == 0),
                                            stop=(f + n == FT))
                    ins.then_inc(filled[bk_], 1)

            t3(0)
            with pe.Fori(0, G - 1) as g:
                gate_up(g)
                t3(g + 1)
                down(g)
            gate_up(G - 1)
            down(G - 1)


def kernel(**inputs):
    import numpy as np
    import concourse.bacc as bacc
    from concourse.bass_utils import run_bass_kernel_spmd

    a = {k: np.asarray(v) for k, v in inputs.items()}

    def per_partition(vector):
        return np.ascontiguousarray(vector.reshape(-1, P).T)

    arrays = {
        "x": a["x"],
        "memT": np.ascontiguousarray(a["ctx_2048"].transpose(0, 2, 1)),
        "mem": a["ctx_2048"],
        "mask": np.ascontiguousarray(a["mask_BxS2_bk0"]).reshape(B * S),
        "wT": np.stack([a["L0_attn_W" + n].T for n in "qkvo"]),
        "bq": per_partition(a["L0_attn_bq"]), "bk": per_partition(a["L0_attn_bk"]),
        "bv": a["L0_attn_bv"], "bo": a["L0_attn_bo"], "slopes": a["L0_attn_alibi_slopes"],
        "gate_w": a["L0_ffn_gate_w"], "up_w": a["L0_ffn_up_w"], "down_w": a["L0_ffn_down_w"],
        "gate_s": per_partition(a["L0_ffn_gate_scale"]), "up_s": per_partition(a["L0_ffn_up_scale"]),
        "down_s": a["L0_ffn_down_scale"],
    }
    nc = bacc.Bacc("TRN2", target_bir_lowering=False, num_devices=1)
    arrays = {f"in_{k}": np.ascontiguousarray(v) for k, v in arrays.items()}
    args = [nc.dram_tensor(k, v.shape, mybir.dt.from_np(v.dtype), kind="ExternalInput").ap()
            for k, v in arrays.items()]
    out = nc.dram_tensor("out", (B, S, D), F32, kind="ExternalOutput").ap()
    build(nc, *args, out)
    r = run_bass_kernel_spmd(nc, [arrays], core_ids=[0])
    return r.results[0]["out"]
```

```python
from contextlib import ExitStack

import concourse.bass as bass
from concourse import mybir

B, S, D, H, F = 16, 128, 512, 16, 1536
HD = D // H
P = 128
KT = D // P
GT = 4
G = B // GT
TG = GT * S
HG = H // 4
FT = F // P
EPS = 1e-5
CAP = 30.0
X_SCALE = float(D) ** -0.5
NEG = 1e30
UNBOUNDED = 3e38

EXPONENT_BITS = 0x7F800000
MIN_NORMAL = 2.0 ** -6
ROUNDER = 1.5 * 2.0 ** 20
TO_NAN = 3.4028234663852886e38 / 464.0

ALU = mybir.AluOpType
ACT = mybir.ActivationFunctionType
AX = mybir.AxisListType
F32 = mybir.dt.float32
F32R = mybir.dt.float32r
U32 = mybir.dt.uint32
U8 = mybir.dt.uint8


def attention_order(g):
    order = []
    if g == 0:
        order += [("T1", i) for i in range(GT)]
    if g < G:
        order += [("V", i) for i in range(GT)]
    if g < G:
        order += [("Q", 0), ("K", 0)]
    if g > 0:
        order += [("WO", i) for i in range(GT)]
    for hg in range(HG):
        for half in range(2):
            if g < G:
                order += before_slot(hg, half)
            order += slot_items(g, 2 * hg + half)
    return order


def before_slot(hg, half):
    if hg + 1 < HG:
        return [("QK"[half], hg + 1)]
    return [("N", i) for i in range(GT)] if half == 0 else []


def is_now(g, n):
    return isinstance(g, int) and g == n


def slot_items(g, k):
    if is_now(g, 0):
        return []
    return [(n, k - lag) for n, lag in (("RO", 4), ("PT", 3), ("XS", 2), ("T2", 1)) if 0 <= k - lag < GT]


FIRST_USES = len(attention_order(0))
LOOP_USES = len(attention_order(1))
NPB = 4
NSB = 2
assert FIRST_USES % NPB == 0 and LOOP_USES % NPB == 0 and 2 * FT % 8 == 0 and 2 * FT % (8 - NPB) == 0
Q_BUFS = 3
SLABS = 3 * HG
HEAD_SLABS = SLABS // 2
SLABS_AT = [range(HEAD_SLABS + k, HEAD_SLABS + k + 1) if k < SLABS - HEAD_SLABS else () for k in range(2 * HG)]


def build(nc, x, memT, mem, mask, wT, bq, bk, bv, bo, slopes, gate_w, up_w, down_w, gate_s, up_s, down_s, out):
    quantized = nc.dram_tensor("quantized", [FT, 3, P, 512], F32).ap()

    with ExitStack() as ctx:
        def sb(name, shape, dt, where=ctx):
            return where.enter_context(nc.sbuf_tensor(name, shape, dt))

        def sem(name):
            return ctx.enter_context(nc.semaphore(name))

        bank = [ctx.enter_context(nc.psum_tensor(f"bank{n}", [P, 512], F32)) for n in range(8)]
        proj_bank, score_bank, ctx_bank, den_bank = bank[0:NPB], bank[NPB:NPB + NSB], bank[6], bank[7]

        x_res = sb("x_res", [P, B, D], F32)
        xn = sb("xn", [P, GT, D], F32)
        identity = sb("identity", [P, P], F32)
        bn = sb("bn", [P, GT, 6], F32)
        mv = sb("mv", [P, GT, 2], F32)
        var_eps = sb("var_eps", [P, GT], F32)
        rstd = sb("rstd", [P, GT], F32)
        minus_half = sb("minus_half", [P, GT], F32)
        gate_c = sb("gate_c", [P, FT], F32)
        up_c = sb("up_c", [P, FT], F32)
        half_gate = sb("half_gate", [P, FT], F32)
        fuse_c = sb("fuse_c", [P, FT], F32)
        R_WO, R_XT, R_CT, R_END = 12288, 16384, 20480, 24576
        reduced = sb("reduced", [P, R_END], F32R)
        w_hi = reduced[:, 0:6144].rearrange("p (m k n) -> p m k n", m=3, k=KT)
        w_lo = reduced[:, 6144:12288].rearrange("p (m k n) -> p m k n", m=3, k=KT)
        wo_hi = reduced[:, R_WO:R_WO + 2048].rearrange("p (k n) -> p k n", k=KT)
        wo_lo = reduced[:, R_WO + 2048:R_XT].rearrange("p (k n) -> p k n", k=KT)
        xT_hi = reduced[:, R_XT:R_XT + 2048].rearrange("p (k n) -> p k n", k=KT)
        xT_lo = reduced[:, R_XT + 2048:R_CT].rearrange("p (k n) -> p k n", k=KT)
        cT_hi = reduced[:, R_CT:R_CT + 2048].rearrange("p (k n) -> p k n", k=KT)
        cT_lo = reduced[:, R_CT + 2048:R_END].rearrange("p (k n) -> p k n", k=KT)
        gu_w = reduced[:, 0:12288].rearrange("p (f w k n) -> p f w k n", f=FT, w=2, k=KT)
        down_q = reduced[:, R_WO:R_WO + 6144].rearrange("p (f n) -> p f n", f=FT)
        FD = (R_XT - R_WO) // 512
        x3 = [(xT_hi, xT_lo)] + [(cT_hi, cT_lo)] * (G - 1)

        att = ExitStack()
        with att:
            qbd = sb("qbd", [P, 4, TG], F32, att)
            kT = sb("kT", [P, TG], F32, att)
            v = sb("v", [P, GT, D], F32, att)
            probs = sb("probs", [P, GT, 4, S], F32, att)
            alibi = sb("alibi", [P, H, S], F32, att)
            q_w = sb("q_w", [P, Q_BUFS, 512], F32, att)
            q_m = sb("q_m", [P, 2, 512], F32, att)
            q_z = sb("q_z", [P, 512], F32, att)
            ctxT = sb("ctxT", [P, TG], F32, att)
            bv_b = sb("bv_b", [P, D], F32, att)
            bo_b = sb("bo_b", [P, D], F32, att)
            x2T = sb("x2T", [P, KT, S], F32, att)
            memT_sb = sb("memT_sb", [P, 2, KT, S], F32, att)
            mem_sb = sb("mem_sb", [P, 2, D], F32, att)
            mask_u8 = sb("mask_u8", [P, B, S], U8, att)
            mask_cap = sb("mask_cap", [P, GT, S], F32, att)
            valid = sb("valid", [P, GT], F32, att)
            x_sc = sb("x_sc", [P, 2, S], F32, att)
            x_pT = sb("x_pT", [P, 2, S], F32, att)
            x_bias = sb("x_bias", [P, 2], F32, att)
            x_den = sb("x_den", [P, 2], F32, att)
            x_rec = sb("x_rec", [P, 2], F32, att)
            x_w = sb("x_w", [P, 2], F32, att)
            bq_c = sb("bq_c", [P, HG], F32, att)
            bk_c = sb("bk_c", [P, HG], F32, att)
            slope_b = sb("slope_b", [P, H], F32, att)
            rel = sb("rel", [P, S], F32, att)
            ones = sb("ones", [P, HD], F32, att)
        ffn = ExitStack()
        with ffn:
            tanh_g = sb("tanh_g", [P, 2, TG], F32, ffn)
            silu2 = sb("silu2", [P, 2, TG], F32, ffn)
            fused = sb("fused", [P, 2, TG], F32, ffn)
            f_parts = sb("f_parts", [P, FT, 2, TG], F32R, ffn)
            f_hi, f_lo = f_parts[:, :, 0], f_parts[:, :, 1]
            y_sb = sb("y_sb", [P, 2, D], F32, ffn)
            down_c = sb("down_c", [P, D], F32, ffn)

        EARLY = 4 * (4 * TG + TG + GT * D + 4 * GT * S + H * S + 512 * (Q_BUFS + 3) + TG + 2 * D)
        LATE_SLICE = (EARLY - 3 * 2 * 4 * TG) // (2 * 4 * TG)

        raw = [x_res[:, GT * (m + 1):GT * (m + 2), :].rearrange("p i n -> p (i n)") for m in range(3)]
        raw += [probs[:].rearrange("p i j s -> p (i j s)")]

        x_first_loaded, x_rest_loaded = sem("x_first_loaded"), sem("x_rest_loaded")
        raw_loaded = [sem(f"raw_loaded{m}") for m in range(4)]
        params_loaded = sem("params_loaded")
        consts_made, identity_made, rel_made = sem("consts_made"), sem("identity_made"), sem("rel_made")
        w_hi_made, w_lo_made = sem("w_hi_made"), sem("w_lo_made")
        qbd_zeroed, alibi_made = sem("qbd_zeroed"), sem("alibi_made")
        fuse_c_made = sem("fuse_c_made")
        bn_done, var_ready, eps_added, rstd_ready, xn_ready = (
            sem("bn_done"), sem("var_ready"), sem("eps_added"), sem("rstd_ready"), sem("xn_ready"))
        proj_filled = [sem(f"proj_filled{n}") for n in range(NPB)]
        proj_drained = [sem(f"proj_drained{n}") for n in range(NPB)]
        xT_hi_ready, v_ready, k_ready, q_ready = (
            sem("xT_hi_ready"), sem("v_ready"), sem("k_ready"), sem("q_ready"))
        scores_filled, biased, tanhed, exped, masked = (
            sem("scores_filled"), sem("biased"), sem("tanhed"), sem("exped"), sem("masked"))
        ctx_filled, recip_done, ctx_normed, ctx_hi, ctx_lo = (
            sem("ctx_filled"), sem("recip_done"), sem("ctx_normed"), sem("ctx_hi"), sem("ctx_lo"))
        bo_added, attn_added = sem("bo_added"), sem("attn_added")
        memT_loaded = [sem(f"memT_loaded{n}") for n in range(2)]
        mem_loaded = [sem(f"mem_loaded{n}") for n in range(2)]
        mask_step, mask_ready = sem("mask_step"), sem("mask_ready")
        xs_step, xs_ready, xs_exped, xs_weight, x2_added = (
            sem("xs_step"), sem("xs_ready"), sem("xs_exped"), sem("xs_weight"), sem("x2_added"))
        q_loaded = [sem(f"q_loaded{n}") for n in range(Q_BUFS)]
        q_stored = [sem(f"q_stored{n}") for n in range(Q_BUFS)]
        q_step, q_prepared, q_rounded, q_pool = sem("q_step"), sem("q_prepared"), sem("q_rounded"), sem("q_pool")
        gu_loaded = [sem(f"gu_loaded{n}") for n in range(FT)]
        down_loaded, down_late_loaded, down_c_loaded = sem("down_loaded"), sem("down_late_loaded"), sem("down_c_loaded")
        filled = [sem(f"filled{n}") for n in range(8)]
        drained = [sem(f"drained{n}") for n in range(8)]
        x3_hi_ready, tanh_ready, f_hi_ready, f_lo_ready = (
            sem("x3_hi_ready"), sem("tanh_ready"), sem("f_hi_ready"), sem("f_lo_ready"))
        y_ready = sem("y_ready")
        y_stored = [sem(f"y_stored{n}") for n in range(2)]

        def proj_use(item, g):
            shape = 0 if is_now(g, 0) else (G if is_now(g, G) else 1)
            at = attention_order(shape).index(item)
            if shape == 0:
                return at % NPB, at // NPB
            return at % NPB, FIRST_USES // NPB + at // NPB + (g - 1) * (LOOP_USES // NPB)

        PROJ_END = 2 * (FIRST_USES + (G - 1) * LOOP_USES + len(attention_order(G))) // NPB

        def epilogue_slot(f, slot):
            if 1 <= f - 1 < 2 * HG:
                slot(f - 1)

        def uses_before(g):
            return FIRST_USES // NPB + (g - 1) * (LOOP_USES // NPB)

        def ffn_use(item, g):
            name, n = item
            if name in "GU" and is_now(g, 0):
                at = 2 * n + "GU".index(name)
                return NPB + at % (8 - NPB), at // (8 - NPB)
            if name == "T3":
                b_, u = n, 4 * (g - 1)
            elif name == "D":
                b_, u = GT + n, 4 * g
            else:
                at = 2 * n + "GU".index(name)
                b_, u = at % 8, 1 + 4 * (g - 1) + at // 8
            return b_, u + (0 if b_ < NPB else 2 * FT // (8 - NPB))

        def t3_use(g, i):
            return ffn_use(("T3", i), g)

        def gu_use(item, g):
            return ffn_use(item, g)

        def token_tile(g, i):
            if isinstance(g, int):
                return x_res[:, g * GT + i, :]
            return x_res[:, bass.ds(g * GT + i, 1), :].rearrange("p a n -> p (a n)")

        def next_group_tile(g, i):
            if isinstance(g, int):
                return token_tile((g + 1) % G, i)
            return x_res[:, bass.ds(((g + 1) % G) * GT + i, 1), :].rearrange("p a n -> p (a n)")

        def wait_apart(e, semaphore, value):
            e.wait_ge(semaphore, value)
            if not isinstance(value, int):
                e.nop(nofuse=True)

        def wait_proj(e, item, g):
            b, n = proj_use(item, g)
            e.wait_ge(proj_filled[b], n + 1)
            return proj_bank[b]

        def proj_sem(item, g):
            return proj_drained[proj_use(item, g)[0]]

        block = ctx.enter_context(nc.Block())

        @block.sync
        def _(sp):
            x_t = x.rearrange("b s d -> s b d")
            sp.dma_start(x_res[:, 0:GT, :], x_t[:, 0:GT, :]).then_inc(x_first_loaded, 16)
            for m in (2, 0, 1, 3):
                sp.dma_start(raw[m].rearrange("p (k n) -> p k n", k=KT),
                             wT[m].rearrange("(k p) n -> p k n", p=P)).then_inc(raw_loaded[m], 16)
            for dst, src in ((bq_c[:], bq), (bk_c[:], bk), (gate_c[:], gate_s), (up_c[:], up_s),
                             (slope_b[:], slopes.partition_broadcast(P)), (bv_b[:], bv.partition_broadcast(P)),
                             (bo_b[:], bo.partition_broadcast(P)),
                             (mask_u8[:].rearrange("p b s -> p (b s)"), mask.partition_broadcast(P))):
                sp.dma_start(dst, src).then_inc(params_loaded, 16)
            sp.wait_ge(w_lo_made, 3)
            sp.dma_start(x_res[:, GT:B, :], x_t[:, GT:B, :]).then_inc(x_rest_loaded, 16)

            def quantize_slab(g, hg, c):
                n = 3 * hg + c
                f = (g - 1) * HG + hg
                src = (gate_w, up_w)[c].rearrange("(k p) (f m) -> f p k m", p=P, m=P) if c < 2 else \
                    down_w.rearrange("(f p) n -> f p n", p=P)
                dst = q_w[:, n % Q_BUFS, :]
                if n >= Q_BUFS:
                    wait_apart(sp, q_stored[n % Q_BUFS], 16 * (n // Q_BUFS) + (g - 1) * (16 * SLABS // Q_BUFS))
                if c < 2:
                    dst = dst.rearrange("p (k m) -> p k m", k=KT)
                    sp.dma_start(dst, src[bass.ds(f, 1)].rearrange("a p k m -> p (a k) m"))\
                        .then_inc(q_loaded[n % Q_BUFS], 16)
                else:
                    sp.dma_start(dst, src[bass.ds(f, 1)].rearrange("a p n -> p (a n)"))\
                        .then_inc(q_loaded[n % Q_BUFS], 16)

            def store_slab(g, hg, c):
                n = 3 * hg + c
                f = (g - 1) * HG + hg
                wait_apart(sp, q_rounded, n + 1 + (g - 1) * 12)
                sp.dma_start(quantized[bass.ds(f, 1), c].rearrange("a p n -> p (a n)"), q_w[:, n % Q_BUFS, :])\
                    .then_inc(q_stored[n % Q_BUFS], 16)

            def load_memT(g, i):
                b = (g - 1) * GT + i
                n = i % 2
                if i >= 2:
                    bk_, u = proj_use(("XS", i - 2), g)
                    wait_apart(sp, proj_filled[bk_], u + 1)
                sp.dma_start(memT_sb[:, n], memT[bass.ds(b, 1)].rearrange("a (k p) m -> p (a k) m", p=P))\
                    .then_inc(memT_loaded[n], 16)

            def load_mem(g, i):
                b = (g - 1) * GT + i
                n = i % 2
                if i >= 2:
                    bk_, u = proj_use(("RO", i - 2), g)
                    wait_apart(sp, proj_filled[bk_], u + 1)
                sp.dma_start(mem_sb[:, n], mem[bass.ds(b, 1)].rearrange("a m d -> m (a d)"))\
                    .then_inc(mem_loaded[n], 16)

            def iteration(g):
                between = {Q_BUFS - 1: [(load_memT, 0), (load_mem, 0), (load_memT, 1), (load_mem, 1)],
                           SLABS - 2: [(load_memT, 2)], SLABS - 1: [(load_memT, 3)]}
                slabs = [(hg, c) for hg in range(HG) for c in range(3)]
                for n, (hg, c) in enumerate(slabs):
                    if n >= Q_BUFS:
                        store_slab(g, *slabs[n - Q_BUFS])
                    quantize_slab(g, hg, c)
                    for load, i in between.get(n, []):
                        load(g, i)
                store_slab(g, *slabs[-3])
                load_mem(g, 2)
                store_slab(g, *slabs[-2])
                load_mem(g, 3)
                store_slab(g, *slabs[-1])
                for i in (2, 3):
                    bk_, u = proj_use(("RO", i), g)
                    wait_apart(sp, proj_filled[bk_], u + 1)
                for n in range(Q_BUFS):
                    wait_apart(sp, q_stored[n], g * (16 * SLABS // Q_BUFS))

            with sp.Fori(1, G) as g:
                iteration(g)
            for i in range(2):
                load_memT(G, i)
                load_mem(G, i)
            b_, u = proj_use(("K", HG - 1), G - 1)
            sp.wait_ge(proj_filled[b_], u + 1)
            between = {7: [(load_memT, 2), (load_memT, 3)], 10: [(load_mem, 2), (load_mem, 3)]}
            for f in range(FT):
                for load, i in between.get(f, []):
                    load(G, i)
                sp.dma_start(gu_w[:, f].rearrange("p w k n -> p w (k n)").bitcast(F32),
                             quantized[f, 0:2].rearrange("w p n -> p w n")).then_inc(gu_loaded[f], 16)
            b_, u = proj_use(("WO", GT - 1), G)
            sp.wait_ge(proj_filled[b_], u + 1)
            sp.dma_start(down_q[:, 0:FD].bitcast(F32), quantized[0:FD, 2].rearrange("f p n -> p f n"))\
                .then_inc(down_loaded, 16)
            b_, u = gu_use(("U", FT - 1), 0)
            sp.wait_ge(filled[b_], u + 1)
            sp.dma_start(down_q[:, FD:].bitcast(F32), quantized[FD:, 2].rearrange("f p n -> p f n"))\
                .then_inc(down_late_loaded, 16)

            for i in (2, 3):
                b_, u = proj_use(("RO", i), G)
                sp.wait_ge(proj_drained[b_], 2 * (u + 1))
            sp.dma_start(down_c[:], down_s.partition_broadcast(P)).then_inc(down_c_loaded, 16)

            def store_out(g):
                for i in range(GT):
                    wait_apart(sp, y_ready, i + 1 + g * GT)
                    sp.dma_start(out[bass.ds(g * GT + i, 1)].rearrange("a s d -> s (a d)"), y_sb[:, i % 2, :])\
                        .then_inc(y_stored[i % 2], 16)

            with sp.Fori(0, G) as g:
                store_out(g)
            sp.wait_ge(y_stored[0], 16 * B // 2)
            sp.wait_ge(y_stored[1], 16 * B // 2)

        @block.gpsimd
        def _(pool):
            pool.memset(identity[:], 0.0).then_inc(consts_made, 1)
            pool.memset(ones[:], 1.0).then_inc(consts_made, 1)
            pool.memset(minus_half[:], -0.5).then_inc(consts_made, 1)
            pool.iota(rel[:], pattern=[[-1, S]], base=0, channel_multiplier=1,
                      allow_small_or_imprecise_dtypes=True).then_inc(rel_made, 1)
            pool.wait_ge(consts_made, 3)
            pool.affine_select(out=identity[:], in_=identity[:], compare_op=ALU.not_equal, fill=1.0,
                               base=0, pattern=[[-1, P]], channel_multiplier=1).then_inc(identity_made, 1)

            def norm_scale(n):
                wait_apart(pool, var_ready, n * GT + GT)
                pool.tensor_scalar(var_eps[:], mv[:, :, 1], EPS, 1.0, ALU.add, ALU.mult).then_inc(eps_added, 1)
                pool.wait_ge(eps_added, n + 1)
                pool.tensor_tensor(rstd[:], var_eps[:], minus_half[:], ALU.pow).then_inc(rstd_ready, 1)

            def low_part(g, hg):
                m = g * HG + hg
                pool.wait_ge(ctx_hi, m + 1)
                pool.tensor_tensor(cT_lo[:, hg, :], ctxT[:], cT_hi[:, hg, :].bitcast(F32), ALU.subtract)\
                    .then_inc(ctx_lo, 1)

            def causal(g, hg):
                for i in range(GT):
                    wait_apart(pool, exped, (g * HG + hg) * GT + i + 1)
                    pool.affine_select(out=probs[:, i], in_=probs[:, i], compare_op=ALU.is_ge, fill=0.0,
                                       base=0, pattern=[[0, 4], [1, S]], channel_multiplier=-1).then_inc(masked, 1)

            def round_slab(g, n):
                w, m = q_w[:, n % Q_BUFS, :], q_m[:, n % 2, :]
                at = (g - 1) * SLABS + n
                pool.wait_ge(q_prepared, 2 * at + 2)
                pool.tensor_tensor(w, w, m, ALU.add).then_inc(q_pool, 1)
                pool.wait_ge(q_pool, at + 1)
                pool.tensor_tensor(w, w, m, ALU.subtract).then_inc(q_rounded, 1)

            def rounds(g, slabs):
                if not is_now(g, 0):
                    for n in slabs:
                        round_slab(g, n)

            def add_bo(g, tiles=range(GT)):
                for i in tiles:
                    wait_apart(pool, xn_ready, (GT if is_now(g, 0) else 2 * g * GT))
                    pool.tensor_tensor(token_tile(g, i), token_tile(g, i), bo_b[:], ALU.add).then_inc(bo_added, 1)

            def heads(g):
                for hg in range(HG):
                    if is_now(g, 0) and hg == 1:
                        pool.wait_ge(params_loaded, 16 * 8)
                        add_bo(0)
                    causal(g, hg)
                    if hg > 0:
                        low_part(g, hg - 1)
                    rounds(g, SLABS_AT[2 * hg])
                    if hg == 2:
                        norm_scale(2 * g + 1)
                    rounds(g, SLABS_AT[2 * hg + 1])

            norm_scale(0)
            heads(0)
            with pool.Fori(1, G) as g:
                low_part(g - 1, HG - 1)
                rounds(g, (0, 1))
                add_bo(g, (0, 1))
                rounds(g, (2, 3))
                add_bo(g, (2, 3))
                rounds(g, (4, 5))
                norm_scale(2 * g)
                heads(g)
            low_part(G - 1, HG - 1)
            norm_scale(2 * G)

            def ffn_lows(g):
                for f in range(FT):
                    pool.wait_ge(f_hi_ready, g * FT + f + 1)
                    pool.tensor_tensor(f_lo[:, f, :], fused[:, f % 2, :], f_hi[:, f, :].bitcast(F32),
                                       ALU.subtract).then_inc(f_lo_ready, 1)

            ffn_lows(0)
            norm_scale(2 * G + 1)
            with pool.Fori(1, G - 1) as g:
                norm_scale(g + 2 * G + 1)
                ffn_lows(g)
            ffn_lows(G - 1)

        @block.scalar
        def _(act):
            for n, m in enumerate((2, 0, 1, 3)):
                act.wait_ge(raw_loaded[m], 16)
                dst = w_hi[:, m] if m < 3 else wo_hi
                act.activation(dst.rearrange("p k n -> p (k n)"), raw[m], ACT.Copy).then_inc(w_hi_made, 1)

            def x_high(name, i, g):
                src = wait_proj(act, (name, i), g)
                act.activation(xT_hi[:, :, i * S:(i + 1) * S], src[:].rearrange("p (k s) -> p k s", k=KT),
                               ACT.Copy).then_inc(xT_hi_ready, 1)

            def k_out(g, hg):
                src = wait_proj(act, ("K", hg), g)
                act.activation(kT[:], src[:], ACT.Identity, bias=bk_c[:, hg:hg + 1])\
                    .then_inc(proj_sem(("K", hg), g), 2)

            def q_out(g, hg):
                src = wait_proj(act, ("Q", hg), g)
                if is_now(g, 0) and hg == 0:
                    act.wait_ge(qbd_zeroed, 1)
                    act.wait_ge(params_loaded, 16 * 8)
                for j in range(4):
                    rows = slice(HD * j, HD * (j + 1))
                    ins = act.activation(qbd[rows, j, :], src[rows, :], ACT.Identity, bias=bq_c[rows, hg:hg + 1])
                ins.then_inc(proj_sem(("Q", hg), g), 2)

            def softmax_terms(g, hg):
                def tanh(i):
                    act.wait_ge(biased, (g * HG + hg) * GT + i + 1)
                    act.activation(probs[:, i], probs[:, i], ACT.Tanh, scale=1.0 / (float(HD) ** 0.5 * CAP))\
                        .then_inc(tanhed, 1)

                def exp(i):
                    act.wait_ge(tanhed, (g * HG + hg) * GT + i + 1)
                    act.activation(probs[:, i], probs[:, i], ACT.Exp, scale=CAP).then_inc(exped, 1)

                tanh(0)
                for i in range(1, GT):
                    tanh(i)
                    exp(i - 1)
                exp(GT - 1)

            def context_high(g, hg):
                act.wait_ge(ctx_normed, g * HG + hg + 1)
                act.activation(cT_hi[:, hg, :], ctxT[:], ACT.Copy).then_inc(ctx_hi, 1)

            def slot(g, k):
                for name, i in slot_items(g, k):
                    n = i % 2
                    at = (g - 1) * GT + i
                    if name == "PT":
                        src = wait_proj(act, ("PT", i), g)
                        act.activation(x_pT[:, n, :], src[:, 0:S], ACT.Copy).then_inc(proj_sem(("PT", i), g), 2)
                    if name == "XS":
                        act.wait_ge(xs_ready, at + 1)
                        act.activation(x_sc[:, n, :], x_sc[:, n, :], ACT.Exp, bias=x_bias[:, n:n + 1],
                                       accum_out=x_den[:, n:n + 1]).then_inc(xs_exped, 1)
                    if name == "T2":
                        src = wait_proj(act, ("T2", i), g)
                        act.activation(x2T[:].rearrange("p k s -> p (k s)"), src[:], ACT.Copy)\
                            .then_inc(proj_sem(("T2", i), g), 2)

            def heads(g):
                q_out(g, 0)
                k_out(g, 0)
                for hg in range(HG):
                    softmax_terms(g, hg)
                    for half in range(2):
                        for name, i in before_slot(hg, half):
                            if name == "Q":
                                q_out(g, i)
                            if name == "K":
                                k_out(g, i)
                            if name == "N":
                                x_high("N", i, g)
                        if half == 0 and hg > 0:
                            context_high(g, hg - 1)
                        slot(g, 2 * hg + half)

            for i in range(GT):
                x_high("T1", i, 0)
            heads(0)
            with act.Fori(1, G) as g:
                context_high(g - 1, HG - 1)
                heads(g)
            context_high(G - 1, HG - 1)

            def x3_high(g):
                for i in range(GT):
                    bk_, u = t3_use(g, i)
                    act.wait_ge(filled[bk_], u + 1)
                    act.activation(cT_hi[:, :, i * S:(i + 1) * S], bank[bk_][:].rearrange("p (k s) -> p k s", k=KT),
                                   ACT.Copy).then_inc(x3_hi_ready, 1)

            def high(g, f):
                bk_, u = gu_use(("U", f), g)
                act.wait_ge(drained[bk_], 2 * (u + 1))
                if is_now(g, 0) and f == LATE_SLICE:
                    for b_ in range(NPB):
                        act.wait_ge(proj_drained[b_], PROJ_END)
                act.activation(f_hi[:, f, :], fused[:, f % 2, :], ACT.Copy).then_inc(f_hi_ready, 1)

            def gates(g):
                for f in range(FT):
                    bk_, u = gu_use(("G", f), g)
                    act.wait_ge(filled[bk_], u + 1)
                    act.activation(tanh_g[:, f % 2, :], bank[bk_][:], ACT.Tanh, scale=half_gate[:, f:f + 1])\
                        .then_inc(tanh_ready, 1)
                    if f >= 1:
                        high(g, f - 1)
                    if is_now(g, 0):
                        epilogue_slot(f, lambda k: slot(G, k))
                high(g, FT - 1)

            act.wait_ge(fuse_c_made, 3)
            gates(0)
            x3_high(1)
            with act.Fori(1, G - 1) as g:
                gates(g)
                x3_high(g + 1)
            gates(G - 1)

        @block.vector
        def _(dve):
            def norm_stats(n, i, tile):
                dve.bn_stats(bn[:, i, :], tile).then_inc(bn_done, 1)

            def norm_moments(n):
                for i in range(GT):
                    wait_apart(dve, bn_done, n * GT + i + 1)
                    dve.bn_aggr(mv[:, i, :], bn[:, i, :]).then_inc(var_ready, 1)

            def norm_apply(n, tile):
                dve.wait_ge(rstd_ready, n + 1)
                for i in range(GT):
                    dve.tensor_scalar(xn[:, i, :], tile(i), mv[:, i, 0:1], rstd[:, i:i + 1], ALU.subtract,
                                      ALU.mult).then_inc(xn_ready, 1)

            def norm(n, tile):
                for i in range(GT):
                    norm_stats(n, i, tile(i))
                norm_moments(n)
                norm_apply(n, tile)

            def x_low(name, i, g):
                b_, u = proj_use((name, i), g)
                dve.wait_ge(xT_hi_ready, GT * (g + (name == "N")) + i + 1)
                dve.tensor_tensor(xT_lo[:, :, i * S:(i + 1) * S], proj_bank[b_][:].rearrange("p (k s) -> p k s", k=KT),
                                  xT_hi[:, :, i * S:(i + 1) * S].bitcast(F32), ALU.subtract)\
                    .then_inc(proj_drained[b_], 2)

            def v_out(g, tiles=range(GT)):
                for i in tiles:
                    src = wait_proj(dve, ("V", i), g)
                    dve.tensor_tensor(v[:, i, :], src[:], bv_b[:], ALU.add).then_inc(proj_sem(("V", i), g), 2)

            def wo_out(g, tiles=range(GT)):
                for i in tiles:
                    src = wait_proj(dve, ("WO", i), g)
                    t = token_tile(g - 1, i)
                    dve.wait_ge(bo_added, (g - 1) * GT + i + 1)
                    dve.tensor_tensor(t, src[:], t, ALU.add).then_inc(proj_sem(("WO", i), g), 2)
                    b_, u = proj_use(("WO", i), g)
                    wait_apart(dve, proj_drained[b_], 2 * (u + 1))
                    norm_stats(2 * g, i, t)

            def alibi_add(g, hg):
                m = g * HG + hg
                for i in range(GT):
                    dve.wait_ge(scores_filled, m * GT + i + 1)
                    dve.tensor_tensor(probs[:, i].rearrange("p j s -> p (j s)"), score_bank[i % NSB][:],
                                      alibi[:, 4 * hg:4 * hg + 4].rearrange("p j s -> p (j s)"), ALU.add)\
                        .then_inc(biased, 1)

            def normalize_context(g, hg):
                m = g * HG + hg
                dve.wait_ge(ctx_filled, m + 1)
                if not (is_now(g, 0) and hg == 0):
                    dve.wait_ge(ctx_lo, m)
                dve.reciprocal(ctxT[:], den_bank[:]).then_inc(recip_done, 1)
                dve.wait_ge(recip_done, m + 1)
                dve.tensor_tensor(ctxT[:], ctx_bank[:], ctxT[:], ALU.mult).then_inc(ctx_normed, 1)

            def masks(g):
                at = g - 1
                dve.tensor_copy(mask_cap[:], mask_u8[:, bass.ds(at * GT, GT), :]).then_inc(mask_step, 1)
                dve.wait_ge(mask_step, 1 + at)
                dve.tensor_reduce(valid[:], mask_cap[:], AX.X, ALU.max).then_inc(mask_ready, 1)
                wait_apart(dve, mask_ready, 2 * at + 1)
                dve.tensor_scalar(mask_cap[:], mask_cap[:], UNBOUNDED, -NEG, ALU.mult, ALU.add).then_inc(mask_ready, 1)

            def slot(g, k):
                for name, i in slot_items(g, k):
                    n = i % 2
                    at = (g - 1) * GT + i
                    if name == "XS":
                        src = wait_proj(dve, ("XS", i), g)
                        dve.wait_ge(mask_ready, 2 * g)
                        dve.scalar_tensor_tensor(x_sc[:, n, :], src[:, 0:S], X_SCALE, mask_cap[:, i, :], ALU.mult,
                                                 ALU.min).then_inc(proj_sem(("XS", i), g), 2)
                        b_, u = proj_use(("XS", i), g)
                        dve.wait_ge(proj_drained[b_], 2 * (u + 1))
                        dve.tensor_reduce(x_bias[:, n:n + 1], x_sc[:, n, :], AX.X, ALU.max, negate=True)\
                            .then_inc(xs_ready, 1)
                    if name == "RO":
                        dve.wait_ge(xs_exped, at + 1)
                        dve.reciprocal(x_rec[:, n:n + 1], x_den[:, n:n + 1]).then_inc(xs_weight, 1)
                        dve.wait_ge(xs_weight, 2 * at + 1)
                        dve.tensor_tensor(x_w[:, n:n + 1], x_rec[:, n:n + 1], valid[:, i:i + 1], ALU.mult)\
                            .then_inc(xs_weight, 1)
                        dve.wait_ge(xs_weight, 2 * at + 2)
                        src = wait_proj(dve, ("RO", i), g)
                        t = token_tile(g - 1, i)
                        dve.scalar_tensor_tensor(t, src[:], x_w[:, n:n + 1], t, ALU.mult, ALU.add)\
                            .then_inc(proj_sem(("RO", i), g), 2)

            def prepare_slab(g, n):
                at = (g - 1) * SLABS + n
                w, m, z = q_w[:, n % Q_BUFS, :], q_m[:, n % 2, :], q_z[:]
                dve.wait_ge(q_loaded[n % Q_BUFS], 16 * (n // Q_BUFS + 1) + (g - 1) * (16 * SLABS // Q_BUFS))
                if n > 0:
                    dve.wait_ge(q_prepared, 2 * at)
                if n > 1:
                    dve.wait_ge(q_rounded, at - 1)
                dve.tensor_scalar(m.bitcast(U32), w.bitcast(U32), EXPONENT_BITS, None, ALU.bitwise_and)\
                    .then_inc(q_step, 1)
                dve.tensor_scalar(z, w, TO_NAN, 0.0, ALU.mult, ALU.mult).then_inc(q_step, 1)
                dve.wait_ge(q_step, 2 * at + 2)
                dve.tensor_scalar(m, m, MIN_NORMAL, ROUNDER, ALU.max, ALU.mult).then_inc(q_prepared, 1)
                dve.tensor_tensor(w, w, z, ALU.add).then_inc(q_prepared, 1)

            def prepares(g, slabs):
                if not is_now(g, 0):
                    for n in slabs:
                        prepare_slab(g, n)

            def heads(g):
                def next_tile(i):
                    return next_group_tile(g, i)

                for hg in range(HG):
                    alibi_add(g, hg)
                    if hg > 0:
                        normalize_context(g, hg - 1)
                    elif not is_now(g, 0):
                        norm_moments(2 * g)
                        masks(g)
                        norm_apply(2 * g, lambda i: token_tile(g - 1, i))
                    for half in range(2):
                        for name, i in before_slot(hg, half):
                            if name == "N":
                                x_low("N", i, g)
                        slot(g, 2 * hg + half)
                        prepares(g, SLABS_AT[2 * hg + half])
                        if hg == 2 and half == 0:
                            if is_now(g, 0):
                                dve.wait_ge(x_rest_loaded, 16)
                            for i in range(GT):
                                norm_stats(2 * g + 1, i, next_tile(i))
                            norm_moments(2 * g + 1)
                        if hg == 2 and half == 1:
                            if not is_now(g, 0):
                                wait_proj(dve, ("T2", GT - 1), g)
                            norm_apply(2 * g + 1, next_tile)

            dve.wait_ge(x_first_loaded, 16)
            norm(0, lambda i: token_tile(0, i))
            for n, m in enumerate((2, 0, 1, 3)):
                if n == 3:
                    v_out(0)
                dve.wait_ge(w_hi_made, n + 1)
                hi, lo = (w_hi[:, m], w_lo[:, m]) if m < 3 else (wo_hi, wo_lo)
                dve.tensor_tensor(lo.rearrange("p k n -> p (k n)"), raw[m],
                                  hi.rearrange("p k n -> p (k n)").bitcast(F32), ALU.subtract)\
                    .then_inc(w_lo_made, 1)
                if n == 0:
                    for i in range(GT):
                        x_low("T1", i, 0)
                    dve.wait_ge(params_loaded, 16 * 8)
            dve.memset(qbd[:], 0.0).then_inc(qbd_zeroed, 1)
            dve.wait_ge(rel_made, 1)
            for h in range(H):
                ins = dve.tensor_scalar(alibi[:, h, :], rel[:], slope_b[:, h:h + 1], None, ALU.mult)
            ins.then_inc(alibi_made, 1)
            dve.tensor_scalar(half_gate[:], gate_c[:], 0.5, None, ALU.mult).then_inc(fuse_c_made, 1)
            dve.tensor_tensor(fuse_c[:], gate_c[:], up_c[:], ALU.mult).then_inc(fuse_c_made, 1)
            dve.wait_ge(fuse_c_made, 2)
            dve.tensor_scalar(fuse_c[:], fuse_c[:], 0.5, None, ALU.mult).then_inc(fuse_c_made, 1)
            dve.wait_ge(alibi_made, 1)
            heads(0)
            with dve.Fori(1, G) as g:
                normalize_context(g - 1, HG - 1)
                v_out(g, (0, 1))
                prepares(g, (0,))
                v_out(g, (2,))
                prepares(g, (1,))
                v_out(g, (3,))
                prepares(g, (2, 3))
                wo_out(g, (0,))
                prepares(g, (4,))
                wo_out(g, (1, 2))
                prepares(g, (5,))
                wo_out(g, (3,))
                heads(g)
            normalize_context(G - 1, HG - 1)
            wo_out(G)
            norm_moments(2 * G)
            masks(G)

            def x3_low(g):
                for i in range(GT):
                    bk_, u = t3_use(g, i)
                    dve.wait_ge(x3_hi_ready, (g - 1) * GT + i + 1)
                    dve.tensor_tensor(cT_lo[:, :, i * S:(i + 1) * S], bank[bk_][:].rearrange("p (k s) -> p k s", k=KT),
                                      cT_hi[:, :, i * S:(i + 1) * S].bitcast(F32), ALU.subtract)\
                        .then_inc(drained[bk_], 2)

            def fuse(g):
                for f in range(FT):
                    at = g * FT + f
                    bg, ug = gu_use(("G", f), g)
                    bu, uu = gu_use(("U", f), g)
                    dve.wait_ge(tanh_ready, at + 1)
                    dve.scalar_tensor_tensor(silu2[:, f % 2, :], tanh_g[:, f % 2, :], 1.0, bank[bg][:], ALU.add, ALU.mult)\
                        .then_inc(drained[bg], 2)
                    dve.wait_ge(drained[bg], 2 * (ug + 1))
                    dve.wait_ge(filled[bu], uu + 1)
                    if f >= 2:
                        dve.wait_ge(f_lo_ready, at - 1)
                    dve.scalar_tensor_tensor(fused[:, f % 2, :], bank[bu][:], fuse_c[:, f:f + 1], silu2[:, f % 2, :],
                                             ALU.mult, ALU.mult).then_inc(drained[bu], 2)
                    if is_now(g, 0):
                        if f == 0:
                            norm_apply(2 * G, lambda i: token_tile(G - 1, i))
                        epilogue_slot(f, lambda k: slot(G, k))

            def y_out(g):
                dve.wait_ge(down_c_loaded, 16)
                for i in range(GT):
                    bk_, u = gu_use(("D", i), g)
                    at = g * GT + i
                    dve.wait_ge(filled[bk_], u + 1)
                    if i >= 2:
                        dve.wait_ge(y_stored[i % 2], 16 * (i // 2) + g * 32)
                    elif not is_now(g, 0):
                        dve.wait_ge(y_stored[i % 2], g * 32)
                    dve.tensor_tensor(y_sb[:, i % 2, :], bank[bk_][:], down_c[:], ALU.mult).then_inc(drained[bk_], 2)
                    dve.wait_ge(drained[bk_], 2 * (u + 1))
                    dve.tensor_tensor(y_sb[:, i % 2, :], y_sb[:, i % 2, :], token_tile(g, i), ALU.add)\
                        .then_inc(y_ready, 1)

            fuse(0)
            norm(2 * G + 1, lambda i: token_tile(1, i))
            x3_low(1)
            y_out(0)
            with dve.Fori(1, G - 1) as g:
                norm(g + 2 * G + 1, lambda i: token_tile(g + 1, i))
                fuse(g)
                x3_low(g + 1)
                y_out(g)
            fuse(G - 1)
            y_out(G - 1)

        @block.tensor
        def _(pe):
            def take(item, g):
                b_, u = proj_use(item, g)
                if not (is_now(g, 0) and u == 0):
                    pe.wait_ge(proj_drained[b_], 2 * u)
                return proj_bank[b_], proj_filled[b_]

            def transposes(dst, n, i):
                pe.wait_ge(xn_ready, n * GT + i + 1)
                for k in range(KT):
                    ins = pe.transpose(dst[:, k * S:(k + 1) * S], xn[:, i, k * P:(k + 1) * P], identity[:])
                return ins

            def t1(name, i, g, n):
                dst, done = take((name, i), g)
                transposes(dst, n, i).then_inc(done, 1)

            def products(dst, pairs):
                for n, (stationary, moving) in enumerate(pairs):
                    ins = pe.matmul(dst, stationary, moving, start=(n == 0), stop=(n == len(pairs) - 1))
                return ins

            def v_proj(g):
                for b_ in range(NPB):
                    pe.wait_ge(proj_drained[b_], 2 * GT // NPB if is_now(g, 0) else 2 * uses_before(g))
                for i in range(GT):
                    dst, done = take(("V", i), g)
                    t = slice(i * S, (i + 1) * S)
                    products(dst[:], [p for k in range(KT) for p in (
                        (xT_hi[:, k, t], w_hi[:, 2, k]), (xT_hi[:, k, t], w_lo[:, 2, k]),
                        (xT_lo[:, k, t], w_hi[:, 2, k]))]).then_inc(done, 1)

            def wo_proj(g):
                pe.wait_ge(ctx_lo, g * HG)
                for i in range(GT):
                    dst, done = take(("WO", i), g)
                    t = slice(i * S, (i + 1) * S)
                    products(dst[:], [p for k in range(KT) for p in (
                        (cT_hi[:, k, t], wo_hi[:, k]), (cT_hi[:, k, t], wo_lo[:, k]),
                        (cT_lo[:, k, t], wo_hi[:, k]))]).then_inc(done, 1)

            def qk_proj(g, name, hg):
                m = "QK".index(name)
                dst, done = take((name, hg), g)
                n = slice(hg * P, (hg + 1) * P)
                products(dst[:], [p for k in range(KT) for p in (
                    (w_hi[:, m, k, n], xT_hi[:, k]), (w_hi[:, m, k, n], xT_lo[:, k]),
                    (w_lo[:, m, k, n], xT_hi[:, k]))]).then_inc(done, 1)

            def scores(g, hg):
                m = g * HG + hg
                for name in ("Q", "K"):
                    b_, u = proj_use((name, hg), g)
                    pe.wait_ge(proj_drained[b_], 2 * (u + 1))
                for i in range(GT):
                    t = slice(i * S, (i + 1) * S)
                    if not (is_now(g, 0) and hg == 0 and i < NSB):
                        pe.wait_ge(biased, m * GT - NSB + i + 1)
                    pe.matmul(score_bank[i % NSB][:], kT[:, t], qbd[:, :, t], start=True, stop=True)\
                        .then_inc(scores_filled, 1)

            def context(g, hg):
                m = g * HG + hg
                if not (is_now(g, 0) and hg == 0):
                    pe.wait_ge(ctx_normed, m)
                if hg == 0:
                    b_, u = proj_use(("V", GT - 1), g)
                    pe.wait_ge(proj_drained[b_], 2 * (u + 1))
                    b_, u = proj_use(("V", GT - 2), g)
                    pe.wait_ge(proj_drained[b_], 2 * (u + 1))
                for i in range(GT):
                    t = slice(i * S, (i + 1) * S)
                    pe.wait_ge(masked, m * GT + i + 1)
                    for j in range(4):
                        rows = slice(HD * j, HD * (j + 1))
                        col = hg * P + HD * j
                        pe.matmul(ctx_bank[rows, t], v[:, i, col:col + HD], probs[:, i, j, :], start=True, stop=True)
                    for j in range(4):
                        rows = slice(HD * j, HD * (j + 1))
                        ins = pe.matmul(den_bank[rows, t], ones[:], probs[:, i, j, :], start=True, stop=True)
                ins.then_inc(ctx_filled, 1)

            def slot(g, k):
                for name, i in slot_items(g, k):
                    n = i % 2
                    dst, done = take((name, i), g)
                    if name == "T2":
                        transposes(dst, 2 * g, i).then_inc(done, 1)
                    if name == "XS":
                        b_, u = proj_use(("T2", i), g)
                        pe.wait_ge(proj_drained[b_], 2 * (u + 1))
                        pe.wait_ge(memT_loaded[n], 16 * (i // 2 + 1) + (g - 1) * 32)
                        products(dst[:, 0:S], [(x2T[:, k_, :], memT_sb[:, n, k_, :]) for k_ in range(KT)])\
                            .then_inc(done, 1)
                    if name == "PT":
                        pe.wait_ge(xs_exped, (g - 1) * GT + i + 1)
                        pe.transpose(dst[:, 0:S], x_sc[:, n, :], identity[:]).then_inc(done, 1)
                    if name == "RO":
                        b_, u = proj_use(("PT", i), g)
                        pe.wait_ge(proj_drained[b_], 2 * (u + 1))
                        pe.wait_ge(mem_loaded[n], 16 * (i // 2 + 1) + (g - 1) * 32)
                        pe.matmul(dst[:], x_pT[:, n, :], mem_sb[:, n, :], start=True, stop=True).then_inc(done, 1)

            def heads(g):
                for hg in range(HG):
                    scores(g, hg)
                    for half in range(2):
                        for name, i in before_slot(hg, half):
                            if name == "N":
                                t1("N", i, g, 2 * g + 1)
                            else:
                                qk_proj(g, name, i)
                        if hg + 1 == HG and half == 0:
                            context(g, hg)
                        slot(g, 2 * hg + half)
                    if hg + 1 < HG:
                        context(g, hg)

            pe.wait_ge(identity_made, 1)
            for i in range(GT):
                t1("T1", i, 0, 0)
            pe.wait_ge(w_lo_made, 1)
            v_proj(0)
            pe.wait_ge(w_lo_made, 3)
            for name in "QK":
                qk_proj(0, name, 0)
            heads(0)
            with pe.Fori(1, G) as g:
                v_proj(g)
                for name in "QK":
                    qk_proj(g, name, 0)
                wo_proj(g)
                heads(g)
            wo_proj(G)
            pe.wait_ge(biased, G * HG * GT)
            pe.wait_ge(ctx_normed, G * HG)

            def ffn_take(bk_, u):
                if not (isinstance(u, int) and u == 0):
                    pe.wait_ge(drained[bk_], 2 * u)
                return bank[bk_]

            def t3(g):
                for i in range(GT):
                    bk_, u = t3_use(g, i)
                    dst = ffn_take(bk_, u)
                    transposes(dst, g + 2 * G, i).then_inc(filled[bk_], 1)

            def gate_up(g):
                for i in range(GT if not is_now(g, 0) else 0):
                    bk_, u = t3_use(g, i)
                    pe.wait_ge(drained[bk_], 2 * (u + 1))
                if is_now(g, 0):
                    for b_ in range(NPB):
                        pe.wait_ge(proj_drained[b_], 2 * uses_before(G))
                for f in range(FT):
                    pe.wait_ge(gu_loaded[f], 16)
                    for w, name in ((0, "G"), (1, "U")):
                        bk_, u = gu_use((name, f), g)
                        dst = ffn_take(bk_, u)
                        products(dst[:], [(gu_w[:, f, w, k], part[:, k]) for k in range(KT) for part in x3[g if is_now(g, 0) else 1]])\
                            .then_inc(filled[bk_], 1)
                    if is_now(g, 0):
                        epilogue_slot(f, lambda k: slot(G, k))

            def down(g):
                for i in range(GT):
                    bk_, u = gu_use(("D", i), g)
                    dst = ffn_take(bk_, u)
                    t = slice(i * S, (i + 1) * S)
                    for f in range(FT):
                        if i == 0:
                            pe.wait_ge(f_lo_ready, g * FT + f + 1)
                        if is_now(g, 0) and i == 0 and f in (0, FD):
                            pe.wait_ge(down_loaded if f == 0 else down_late_loaded, 16)
                        for n, part in enumerate((f_hi, f_lo)):
                            ins = pe.matmul(dst[:], part[:, f, t], down_q[:, f], start=(f + n == 0),
                                            stop=(f + n == FT))
                    ins.then_inc(filled[bk_], 1)

            gate_up(0)
            for b_ in range(NPB):
                pe.wait_ge(proj_drained[b_], PROJ_END)
            t3(1)
            down(0)
            with pe.Fori(1, G - 1) as g:
                gate_up(g)
                t3(g + 1)
                down(g)
            gate_up(G - 1)
            down(G - 1)


def kernel(**inputs):
    import numpy as np
    import concourse.bacc as bacc
    from concourse.bass_utils import run_bass_kernel_spmd

    a = {k: np.asarray(v) for k, v in inputs.items()}

    def per_partition(vector):
        return np.ascontiguousarray(vector.reshape(-1, P).T)

    arrays = {
        "x": a["x"],
        "memT": np.ascontiguousarray(a["ctx_2048"].transpose(0, 2, 1)),
        "mem": a["ctx_2048"],
        "mask": np.ascontiguousarray(a["mask_BxS2_bk0"]).reshape(B * S),
        "wT": np.stack([a["L0_attn_W" + n].T for n in "qkvo"]),
        "bq": per_partition(a["L0_attn_bq"]), "bk": per_partition(a["L0_attn_bk"]),
        "bv": a["L0_attn_bv"], "bo": a["L0_attn_bo"], "slopes": a["L0_attn_alibi_slopes"],
        "gate_w": a["L0_ffn_gate_w"], "up_w": a["L0_ffn_up_w"], "down_w": a["L0_ffn_down_w"],
        "gate_s": per_partition(a["L0_ffn_gate_scale"]), "up_s": per_partition(a["L0_ffn_up_scale"]),
        "down_s": a["L0_ffn_down_scale"],
    }
    nc = bacc.Bacc("TRN2", target_bir_lowering=False, num_devices=1)
    arrays = {f"in_{k}": np.ascontiguousarray(v) for k, v in arrays.items()}
    args = [nc.dram_tensor(k, v.shape, mybir.dt.from_np(v.dtype), kind="ExternalInput").ap()
            for k, v in arrays.items()]
    out = nc.dram_tensor("out", (B, S, D), F32, kind="ExternalOutput").ap()
    build(nc, *args, out)
    r = run_bass_kernel_spmd(nc, [arrays], core_ids=[0])
    return r.results[0]["out"]
```

```python
from contextlib import ExitStack

import concourse.bass as bass
from concourse import mybir

B, S, D, H, F = 16, 128, 512, 16, 1536
HD = D // H
P = 128
KT = D // P
GT = 4
G = B // GT
TG = GT * S
HG = H // 4
FT = F // P
EPS = 1e-5
CAP = 30.0
X_SCALE = float(D) ** -0.5
NEG = 1e30
UNBOUNDED = 3e38

EXPONENT_BITS = 0x7F800000
MIN_NORMAL = 2.0 ** -6
ROUNDER = 1.5 * 2.0 ** 20
TO_ONE = 1.0 / 464.0
TO_RANGE_END = (2.0 - 2.0 ** -22) * 2.0 ** 127

ALU = mybir.AluOpType
ACT = mybir.ActivationFunctionType
AX = mybir.AxisListType
F32 = mybir.dt.float32
F32R = mybir.dt.float32r
U32 = mybir.dt.uint32
U8 = mybir.dt.uint8


def attention_order(g):
    order = []
    if g == 0:
        order += [("T1", i) for i in range(GT)]
    if g < G:
        order += [("V", i) for i in range(GT)]
    if g == 0:
        order += [("Q", 0), ("K", 0)]
    if g > 0:
        order += [("WO", i) for i in range(GT)]
    for k in range(2 * HG):
        if g < G:
            order += before_slot(g, k)
        order += slot_items(g, k)
        if g < G:
            order += after_slot(k)
    return order


def before_slot(g, k):
    if is_now(g, G - 1) and k // 2 + 1 == HG:
        return []
    return [("QK"[k % 2], k // 2 + 1)]


def after_slot(k):
    return [("N", i) for i in range(GT)] if k == 2 * HG - 3 else []


def slabs_at(g, k):
    return () if is_now(g, G - 1) and k >= 2 * HG - len(LATE_SLABS) else SLABS_AT[k]


def is_now(g, n):
    return isinstance(g, int) and g == n


def slot_items(g, k):
    if is_now(g, 0):
        return []
    return [(n, k - lag) for n, lag in (("RO", 4), ("PT", 3), ("XS", 2), ("T2", 1)) if 0 <= k - lag < GT]


FIRST_USES = len(attention_order(0))
LOOP_USES = len(attention_order(1))
NPB = 4
NSB = 2
BEFORE_WO = 2
NORM_AT = 9
LAST_USES = len(attention_order(G - 1))
assert LOOP_USES % NPB == 0 and 2 * FT % 8 == 0 and 2 * FT % (8 - NPB) == 0
Q_BUFS = 3
SLABS = 3 * HG
HEAD_SLABS = SLABS // 3
LATE_SLABS = range(SLABS - 2, SLABS)
SLABS_AT = [range(HEAD_SLABS + k, HEAD_SLABS + k + 1) if k < SLABS - HEAD_SLABS else () for k in range(2 * HG)]


def build(nc, x, memT, mem, mask, wT, bq, bk, bv, bo, slopes, gate_w, up_w, down_w, gate_s, up_s, down_s, out):
    quantized = nc.dram_tensor("quantized", [FT, 3, P, 512], F32).ap()

    with ExitStack() as ctx:
        def sb(name, shape, dt, where=ctx):
            return where.enter_context(nc.sbuf_tensor(name, shape, dt))

        def sem(name):
            return ctx.enter_context(nc.semaphore(name))

        bank = [ctx.enter_context(nc.psum_tensor(f"bank{n}", [P, 512], F32)) for n in range(8)]
        proj_bank, score_bank, ctx_bank, den_bank = bank[0:NPB], bank[NPB:NPB + NSB], bank[6], bank[7]

        x_res = sb("x_res", [P, B, D], F32)
        xn = sb("xn", [P, GT, D], F32)
        identity = sb("identity", [P, P], F32)
        bn = sb("bn", [P, GT, 6], F32)
        mv = sb("mv", [P, GT, 2], F32)
        var_eps = sb("var_eps", [P, GT], F32)
        rstd = sb("rstd", [P, GT], F32)
        minus_half = sb("minus_half", [P, GT], F32)
        gate_c = sb("gate_c", [P, FT], F32)
        up_c = sb("up_c", [P, FT], F32)
        half_gate = sb("half_gate", [P, FT], F32)
        fuse_c = sb("fuse_c", [P, FT], F32)
        R_WO, R_XT, R_CT, R_END = 12288, 16384, 20480, 24576
        reduced = sb("reduced", [P, R_END], F32R)
        w_hi = reduced[:, 0:6144].rearrange("p (m k n) -> p m k n", m=3, k=KT)
        w_lo = reduced[:, 6144:12288].rearrange("p (m k n) -> p m k n", m=3, k=KT)
        wo_hi = reduced[:, R_WO:R_WO + 2048].rearrange("p (k n) -> p k n", k=KT)
        wo_lo = reduced[:, R_WO + 2048:R_XT].rearrange("p (k n) -> p k n", k=KT)
        xT_hi = reduced[:, R_XT:R_XT + 2048].rearrange("p (k n) -> p k n", k=KT)
        xT_lo = reduced[:, R_XT + 2048:R_CT].rearrange("p (k n) -> p k n", k=KT)
        cT_hi = reduced[:, R_CT:R_CT + 2048].rearrange("p (k n) -> p k n", k=KT)
        cT_lo = reduced[:, R_CT + 2048:R_END].rearrange("p (k n) -> p k n", k=KT)
        gu_w = reduced[:, 0:12288].rearrange("p (f w k n) -> p f w k n", f=FT, w=2, k=KT)
        down_q = reduced[:, R_WO:R_WO + 6144].rearrange("p (f n) -> p f n", f=FT)
        FD = (R_XT - R_WO) // 512
        x3 = [(xT_hi, xT_lo)] + [(cT_hi, cT_lo)] * (G - 1)

        att = ExitStack()
        with att:
            qbd = sb("qbd", [P, 4, TG], F32, att)
            kT = sb("kT", [P, TG], F32, att)
            v = sb("v", [P, GT, D], F32, att)
            probs = sb("probs", [P, GT, 4, S], F32, att)
            alibi = sb("alibi", [P, H, S], F32, att)
            q_w = sb("q_w", [P, Q_BUFS, 512], F32, att)
            q_m = sb("q_m", [P, 2, 512], F32, att)
            q_z = sb("q_z", [P, 512], F32, att)
            ctxT = sb("ctxT", [P, TG], F32, att)
            bv_b = sb("bv_b", [P, D], F32, att)
            bo_b = sb("bo_b", [P, D], F32, att)
            x2T = sb("x2T", [P, KT, S], F32, att)
            memT_sb = sb("memT_sb", [P, 2, KT, S], F32, att)
            mem_sb = sb("mem_sb", [P, 2, D], F32, att)
            mask_u8 = sb("mask_u8", [P, B, S], U8, att)
            mask_cap = sb("mask_cap", [P, GT, S], F32, att)
            valid = sb("valid", [P, GT], F32, att)
            x_sc = sb("x_sc", [P, 2, S], F32, att)
            x_pT = sb("x_pT", [P, 2, S], F32, att)
            x_bias = sb("x_bias", [P, 2], F32, att)
            x_den = sb("x_den", [P, 2], F32, att)
            x_rec = sb("x_rec", [P, 2], F32, att)
            x_w = sb("x_w", [P, 2], F32, att)
            bq_c = sb("bq_c", [P, HG], F32, att)
            bk_c = sb("bk_c", [P, HG], F32, att)
            slope_b = sb("slope_b", [P, H], F32, att)
            rel = sb("rel", [P, S], F32, att)
            ones = sb("ones", [P, HD], F32, att)
        ffn = ExitStack()
        with ffn:
            tanh_g = sb("tanh_g", [P, 2, TG], F32, ffn)
            silu2 = sb("silu2", [P, 2, TG], F32, ffn)
            fused = sb("fused", [P, 2, TG], F32, ffn)
            f_parts = sb("f_parts", [P, FT, 2, TG], F32R, ffn)
            f_hi, f_lo = f_parts[:, :, 0], f_parts[:, :, 1]
            y_sb = sb("y_sb", [P, 2, D], F32, ffn)
            down_c = sb("down_c", [P, D], F32, ffn)

        EARLY = 4 * (4 * TG + TG + GT * D + 4 * GT * S + H * S + 512 * (Q_BUFS + 3) + TG + 2 * D)
        LATE_SLICE = (EARLY - 3 * 2 * 4 * TG) // (2 * 4 * TG)

        raw = [x_res[:, GT * (m + 1):GT * (m + 2), :].rearrange("p i n -> p (i n)") for m in range(3)]
        raw += [probs[:].rearrange("p i j s -> p (i j s)")]

        x_first_loaded, x_rest_loaded = [sem(f"x_first_loaded{n}") for n in range(GT)], sem("x_rest_loaded")
        raw_loaded = [sem(f"raw_loaded{m}") for m in range(4)]
        params_loaded = sem("params_loaded")
        consts_made, identity_made, rel_made = sem("consts_made"), sem("identity_made"), sem("rel_made")
        w_hi_made, w_lo_made = sem("w_hi_made"), sem("w_lo_made")
        qbd_zeroed, alibi_made = sem("qbd_zeroed"), sem("alibi_made")
        fuse_c_made = sem("fuse_c_made")
        bn_done, var_ready, eps_added, rstd_ready, xn_ready = (
            sem("bn_done"), sem("var_ready"), sem("eps_added"), sem("rstd_ready"), sem("xn_ready"))
        proj_filled = [sem(f"proj_filled{n}") for n in range(NPB)]
        proj_drained = [sem(f"proj_drained{n}") for n in range(NPB)]
        xT_hi_ready = sem("xT_hi_ready")
        scores_filled, biased, tanhed, exped, masked = (
            sem("scores_filled"), sem("biased"), sem("tanhed"), sem("exped"), sem("masked"))
        ctx_filled, recip_done, ctx_normed, ctx_hi, ctx_lo = (
            sem("ctx_filled"), sem("recip_done"), sem("ctx_normed"), sem("ctx_hi"), sem("ctx_lo"))
        bo_added = sem("bo_added")
        memT_loaded = [sem(f"memT_loaded{n}") for n in range(2)]
        mem_loaded = [sem(f"mem_loaded{n}") for n in range(2)]
        mask_step, mask_ready = sem("mask_step"), sem("mask_ready")
        xs_ready, xs_exped, xs_weight = sem("xs_ready"), sem("xs_exped"), sem("xs_weight")
        q_loaded = [sem(f"q_loaded{n}") for n in range(Q_BUFS)]
        q_stored = [sem(f"q_stored{n}") for n in range(Q_BUFS)]
        q_step, q_prepared, q_rounded, q_pool = sem("q_step"), sem("q_prepared"), sem("q_rounded"), sem("q_pool")
        gu_loaded = [sem(f"gu_loaded{n}") for n in range(FT)]
        down_loaded, down_late_loaded, down_c_loaded = sem("down_loaded"), sem("down_late_loaded"), sem("down_c_loaded")
        filled = [sem(f"filled{n}") for n in range(8)]
        drained = [sem(f"drained{n}") for n in range(8)]
        x3_hi_ready, tanh_ready, f_hi_ready, f_lo_ready = (
            sem("x3_hi_ready"), sem("tanh_ready"), sem("f_hi_ready"), sem("f_lo_ready"))
        y_ready = sem("y_ready")
        y_stored = [sem(f"y_stored{n}") for n in range(2)]

        def proj_use(item, g):
            if isinstance(g, int):
                n = uses_start(g) + attention_order(g).index(item)
                return n % NPB, n // NPB
            n = FIRST_USES + attention_order(1).index(item)
            return n % NPB, n // NPB + (g - 1) * (LOOP_USES // NPB)

        def uses_start(g):
            if g == 0:
                return 0
            return FIRST_USES + (min(g, G - 1) - 1) * LOOP_USES + (LAST_USES if g >= G else 0)

        def uses_before(b_, g):
            return (FIRST_USES + NPB - 1 - b_) // NPB + (g - 1) * (LOOP_USES // NPB)

        PROJ_END = 2 * (uses_start(G) + len(attention_order(G))) // NPB

        def epilogue_slot(f, slot):
            if 1 <= f - 3 < 2 * HG:
                slot(f - 3)

        def ffn_use(item, g):
            name, n = item
            if name in "GU" and is_now(g, 0):
                at = 2 * n + "GU".index(name)
                return NPB + at % (8 - NPB), at // (8 - NPB)
            if name == "T3":
                b_, u = n, 4 * (g - 1)
            elif name == "D":
                b_, u = GT + n, 4 * g
            else:
                at = 2 * n + "GU".index(name)
                b_, u = at % 8, 1 + 4 * (g - 1) + at // 8
            return b_, u + (0 if b_ < NPB else 2 * FT // (8 - NPB))

        def t3_use(g, i):
            return ffn_use(("T3", i), g)

        def gu_use(item, g):
            return ffn_use(item, g)

        def token_tile(g, i):
            if isinstance(g, int):
                return x_res[:, g * GT + i, :]
            return x_res[:, bass.ds(g * GT + i, 1), :].rearrange("p a n -> p (a n)")

        def next_group_tile(g, i):
            return token_tile(0 if is_now(g, G - 1) else g + 1, i)

        def wait_apart(e, semaphore, value):
            e.wait_ge(semaphore, value)
            if not isinstance(value, int):
                e.nop(nofuse=True)

        def wait_proj(e, item, g):
            b, n = proj_use(item, g)
            e.wait_ge(proj_filled[b], n + 1)
            return proj_bank[b]

        def proj_sem(item, g):
            return proj_drained[proj_use(item, g)[0]]

        block = ctx.enter_context(nc.Block())

        @block.sync
        def _(sp):
            x_t = x.rearrange("b s d -> s b d")
            for i in range(GT):
                sp.dma_start(x_res[:, i, :], x_t[:, i, :]).then_inc(x_first_loaded[i], 16)
            for m in (2, 0, 1, 3):
                sp.dma_start(raw[m].rearrange("p (k n) -> p k n", k=KT),
                             wT[m].rearrange("(k p) n -> p k n", p=P)).then_inc(raw_loaded[m], 16)
            for dst, src in ((bq_c[:], bq), (bk_c[:], bk), (gate_c[:], gate_s), (up_c[:], up_s),
                             (slope_b[:], slopes.partition_broadcast(P)), (bv_b[:], bv.partition_broadcast(P)),
                             (bo_b[:], bo.partition_broadcast(P)),
                             (mask_u8[:].rearrange("p b s -> p (b s)"), mask.partition_broadcast(P))):
                sp.dma_start(dst, src).then_inc(params_loaded, 16)
            sp.wait_ge(w_lo_made, 3)
            sp.dma_start(x_res[:, GT:B, :], x_t[:, GT:B, :]).then_inc(x_rest_loaded, 16)

            def quantize_slab(g, hg, c):
                n = 3 * hg + c
                f = (g - 1) * HG + hg
                src = (gate_w, up_w)[c].rearrange("(k p) (f m) -> f p k m", p=P, m=P) if c < 2 else \
                    down_w.rearrange("(f p) n -> f p n", p=P)
                dst = q_w[:, n % Q_BUFS, :]
                if n >= Q_BUFS:
                    wait_apart(sp, q_stored[n % Q_BUFS], 16 * (n // Q_BUFS) + (g - 1) * (16 * SLABS // Q_BUFS))
                if c < 2:
                    dst = dst.rearrange("p (k m) -> p k m", k=KT)
                    sp.dma_start(dst, src[bass.ds(f, 1)].rearrange("a p k m -> p (a k) m"))\
                        .then_inc(q_loaded[n % Q_BUFS], 16)
                else:
                    sp.dma_start(dst, src[bass.ds(f, 1)].rearrange("a p n -> p (a n)"))\
                        .then_inc(q_loaded[n % Q_BUFS], 16)

            def store_slab(g, hg, c):
                n = 3 * hg + c
                f = (g - 1) * HG + hg
                wait_apart(sp, q_rounded, n + 1 + (g - 1) * 12)
                sp.dma_start(quantized[bass.ds(f, 1), c].rearrange("a p n -> p (a n)"), q_w[:, n % Q_BUFS, :])\
                    .then_inc(q_stored[n % Q_BUFS], 16)

            def load_memT(g, i):
                b = (g - 1) * GT + i
                n = i % 2
                if i >= 2:
                    bk_, u = proj_use(("XS", i - 2), g)
                    wait_apart(sp, proj_filled[bk_], u + 1)
                sp.dma_start(memT_sb[:, n], memT[bass.ds(b, 1)].rearrange("a (k p) m -> p (a k) m", p=P))\
                    .then_inc(memT_loaded[n], 16)

            def load_mem(g, i):
                b = (g - 1) * GT + i
                n = i % 2
                if i >= 2:
                    bk_, u = proj_use(("RO", i - 2), g)
                    wait_apart(sp, proj_filled[bk_], u + 1)
                sp.dma_start(mem_sb[:, n], mem[bass.ds(b, 1)].rearrange("a m d -> m (a d)"))\
                    .then_inc(mem_loaded[n], 16)

            def load_gate_up(f):
                sp.dma_start(gu_w[:, f].rearrange("p w k n -> p w (k n)").bitcast(F32),
                             quantized[f, 0:2].rearrange("w p n -> p w n")).then_inc(gu_loaded[f], 16)

            slabs = [(hg, c) for hg in range(HG) for c in range(3)]

            def iteration(g):
                between = {Q_BUFS: [(load_memT, 0), (load_mem, 0), (load_memT, 1), (load_mem, 1)],
                           8: [(load_memT, 2)], 9: [(load_memT, 3)], 10: [(load_mem, 2)], 11: [(load_mem, 3)]}
                for n in range(Q_BUFS, SLABS):
                    for load, i in between.get(n, []) if n == Q_BUFS else []:
                        load(g, i)
                    store_slab(g, *slabs[n - Q_BUFS])
                    quantize_slab(g, *slabs[n])
                    for load, i in between.get(n, []) if n > Q_BUFS else []:
                        load(g, i)
                if is_now(g, G - 1):
                    b_, u = proj_use(("K", HG - 1), g)
                    sp.wait_ge(proj_filled[b_], u + 1)
                for n, slab in enumerate(slabs[-Q_BUFS:]):
                    if is_now(g, G - 1):
                        for f in range(FT - HG)[3 * n:3 * n + 3]:
                            load_gate_up(f)
                    store_slab(g, *slab)
                for n in range(Q_BUFS):
                    wait_apart(sp, q_stored[n], g * (16 * SLABS // Q_BUFS))
                    if not is_now(g, G - 1):
                        quantize_slab(g + 1, *slabs[n])
                for i in (2, 3):
                    bk_, u = proj_use(("RO", i), g)
                    wait_apart(sp, proj_filled[bk_], u + 1)

            for slab in slabs[:Q_BUFS]:
                quantize_slab(1, *slab)
            with sp.Fori(1, G - 1) as g:
                iteration(g)
            iteration(G - 1)
            for i in range(2):
                load_memT(G, i)
                load_mem(G, i)
            load_gate_up(FT - 4)
            load_gate_up(FT - 3)
            load_memT(G, 2)
            load_memT(G, 3)
            load_gate_up(FT - 2)
            load_gate_up(FT - 1)
            load_mem(G, 2)
            load_mem(G, 3)
            b_, u = proj_use(("WO", GT - 1), G)
            sp.wait_ge(proj_filled[b_], u + 1)
            sp.dma_start(down_q[:, 0:FD].bitcast(F32), quantized[0:FD, 2].rearrange("f p n -> p f n"))\
                .then_inc(down_loaded, 16)
            b_, u = gu_use(("U", FT - 1), 0)
            sp.wait_ge(filled[b_], u + 1)
            sp.dma_start(down_q[:, FD:].bitcast(F32), quantized[FD:, 2].rearrange("f p n -> p f n"))\
                .then_inc(down_late_loaded, 16)

            for i in (2, 3):
                b_, u = proj_use(("RO", i), G)
                sp.wait_ge(proj_drained[b_], 2 * (u + 1))
            sp.dma_start(down_c[:], down_s.partition_broadcast(P)).then_inc(down_c_loaded, 16)

            def store_out(g):
                for i in range(GT):
                    wait_apart(sp, y_ready, i + 1 + g * GT)
                    sp.dma_start(out[bass.ds(g * GT + i, 1)].rearrange("a s d -> s (a d)"), y_sb[:, i % 2, :])\
                        .then_inc(y_stored[i % 2], 16)

            with sp.Fori(0, G) as g:
                store_out(g)
            sp.wait_ge(y_stored[0], 16 * B // 2)
            sp.wait_ge(y_stored[1], 16 * B // 2)

        @block.gpsimd
        def _(pool):
            pool.memset(identity[:], 0.0).then_inc(consts_made, 1)
            pool.memset(ones[:], 1.0).then_inc(consts_made, 1)
            pool.memset(minus_half[:], -0.5).then_inc(consts_made, 1)
            pool.iota(rel[:], pattern=[[-1, S]], base=0, channel_multiplier=1,
                      allow_small_or_imprecise_dtypes=True).then_inc(rel_made, 1)
            pool.memset(qbd[:], 0.0).then_inc(qbd_zeroed, 1)
            pool.wait_ge(consts_made, 3)
            pool.affine_select(out=identity[:], in_=identity[:], compare_op=ALU.not_equal, fill=1.0,
                               base=0, pattern=[[-1, P]], channel_multiplier=1).then_inc(identity_made, 1)

            def norm_scale(n):
                wait_apart(pool, var_ready, n * GT + GT)
                pool.tensor_scalar(var_eps[:], mv[:, :, 1], EPS, 1.0, ALU.add, ALU.mult).then_inc(eps_added, 1)
                pool.wait_ge(eps_added, n + 1)
                pool.tensor_tensor(rstd[:], var_eps[:], minus_half[:], ALU.pow).then_inc(rstd_ready, 1)

            def low_part(g, hg):
                m = g * HG + hg
                pool.wait_ge(ctx_hi, m + 1)
                pool.tensor_tensor(cT_lo[:, hg, :], ctxT[:], cT_hi[:, hg, :].bitcast(F32), ALU.subtract)\
                    .then_inc(ctx_lo, 1)

            def causal(g, hg):
                for i in range(GT):
                    wait_apart(pool, exped, (g * HG + hg) * GT + i + 1)
                    pool.affine_select(out=probs[:, i], in_=probs[:, i], compare_op=ALU.is_ge, fill=0.0,
                                       base=0, pattern=[[0, 4], [1, S]], channel_multiplier=-1).then_inc(masked, 1)

            def round_slab(g, n):
                w, m = q_w[:, n % Q_BUFS, :], q_m[:, n % 2, :]
                at = (g - 1) * SLABS + n
                pool.wait_ge(q_prepared, 2 * at + 2)
                pool.tensor_tensor(w, w, m, ALU.add).then_inc(q_pool, 1)
                pool.wait_ge(q_pool, at + 1)
                pool.tensor_tensor(w, w, m, ALU.subtract).then_inc(q_rounded, 1)

            def rounds(g, slabs):
                if not is_now(g, 0):
                    for n in slabs:
                        round_slab(g, n)

            def add_bo(g, tiles=range(GT)):
                for i in tiles:
                    wait_apart(pool, xn_ready, (GT if is_now(g, 0) else 2 * g * GT))
                    pool.tensor_tensor(token_tile(g, i), token_tile(g, i), bo_b[:], ALU.add).then_inc(bo_added, 1)

            def heads(g):
                for hg in range(HG):
                    if is_now(g, 0) and hg == 1:
                        add_bo(0)
                    causal(g, hg)
                    if hg > 0:
                        low_part(g, hg - 1)
                    rounds(g, slabs_at(g, 2 * hg))
                    rounds(g, slabs_at(g, 2 * hg + 1))
                    if hg == 1:
                        norm_scale(2 * g + 1)

            norm_scale(0)
            pool.wait_ge(params_loaded, 16 * 8)
            heads(0)

            def iteration(g):
                low_part(g - 1, HG - 1)
                rounds(g, (0, 1))
                add_bo(g)
                rounds(g, (2, 3))
                norm_scale(2 * g)
                heads(g)

            with pool.Fori(1, G - 1) as g:
                iteration(g)
            iteration(G - 1)
            low_part(G - 1, HG - 1)
            rounds(G - 1, LATE_SLABS)

            def ffn_lows(g):
                for f in range(FT):
                    if is_now(g, 0) and f == BEFORE_WO:
                        norm_scale(2 * G)
                    if is_now(g, 0) and f == NORM_AT:
                        norm_scale(2 * G + 1)
                    pool.wait_ge(f_hi_ready, g * FT + f + 1)
                    pool.tensor_tensor(f_lo[:, f, :], fused[:, f % 2, :], f_hi[:, f, :].bitcast(F32),
                                       ALU.subtract).then_inc(f_lo_ready, 1)

            ffn_lows(0)
            with pool.Fori(1, G - 1) as g:
                norm_scale(g + 2 * G + 1)
                ffn_lows(g)
            ffn_lows(G - 1)

        @block.scalar
        def _(act):
            def weight_high(m):
                act.wait_ge(raw_loaded[m], 16)
                dst = w_hi[:, m] if m < 3 else wo_hi
                act.activation(dst.rearrange("p k n -> p (k n)"), raw[m], ACT.Copy).then_inc(w_hi_made, 1)

            def x_high(name, i, g):
                src = wait_proj(act, (name, i), g)
                act.activation(xT_hi[:, :, i * S:(i + 1) * S], src[:].rearrange("p (k s) -> p k s", k=KT),
                               ACT.Copy).then_inc(xT_hi_ready, 1)

            def k_out(g, hg):
                src = wait_proj(act, ("K", hg), g)
                act.activation(kT[:], src[:], ACT.Identity, bias=bk_c[:, hg % HG:hg % HG + 1])\
                    .then_inc(proj_sem(("K", hg), g), 2)

            def q_out(g, hg):
                src = wait_proj(act, ("Q", hg), g)
                if is_now(g, 0) and hg == 0:
                    act.wait_ge(qbd_zeroed, 1)
                    act.wait_ge(params_loaded, 16 * 8)
                for j in range(4):
                    rows = slice(HD * j, HD * (j + 1))
                    ins = act.activation(qbd[rows, j, :], src[rows, :], ACT.Identity, bias=bq_c[rows, hg % HG:hg % HG + 1])
                ins.then_inc(proj_sem(("Q", hg), g), 2)

            def softmax_terms(g, hg):
                def tanh(i):
                    act.wait_ge(biased, (g * HG + hg) * GT + i + 1)
                    act.activation(probs[:, i], probs[:, i], ACT.Tanh, scale=1.0 / (float(HD) ** 0.5 * CAP))\
                        .then_inc(tanhed, 1)

                def exp(i):
                    act.wait_ge(tanhed, (g * HG + hg) * GT + i + 1)
                    act.activation(probs[:, i], probs[:, i], ACT.Exp, scale=CAP).then_inc(exped, 1)

                tanh(0)
                for i in range(1, GT):
                    tanh(i)
                    exp(i - 1)
                exp(GT - 1)

            def context_high(g, hg):
                act.wait_ge(ctx_normed, g * HG + hg + 1)
                act.activation(cT_hi[:, hg, :], ctxT[:], ACT.Copy).then_inc(ctx_hi, 1)

            def slot(g, k):
                for name, i in slot_items(g, k):
                    n = i % 2
                    at = (g - 1) * GT + i
                    if name == "PT":
                        src = wait_proj(act, ("PT", i), g)
                        act.activation(x_pT[:, n, :], src[:, 0:S], ACT.Copy).then_inc(proj_sem(("PT", i), g), 2)
                    if name == "XS":
                        act.wait_ge(xs_ready, at + 1)
                        act.activation(x_sc[:, n, :], x_sc[:, n, :], ACT.Exp, bias=x_bias[:, n:n + 1],
                                       accum_out=x_den[:, n:n + 1]).then_inc(xs_exped, 1)
                    if name == "T2":
                        src = wait_proj(act, ("T2", i), g)
                        act.activation(x2T[:].rearrange("p k s -> p (k s)"), src[:], ACT.Copy)\
                            .then_inc(proj_sem(("T2", i), g), 2)

            def heads(g):
                for hg in range(HG):
                    softmax_terms(g, hg)
                    for k in (2 * hg, 2 * hg + 1):
                        for name, i in before_slot(g, k):
                            (q_out if name == "Q" else k_out)(g, i)
                        slot(g, k)
                        if k % 2 == 0 and hg > 0:
                            context_high(g, hg - 1)
                        for name, i in after_slot(k):
                            x_high(name, i, g)

            weight_high(2)
            for i in range(GT):
                x_high("T1", i, 0)
            for m in (0, 1, 3):
                weight_high(m)
            q_out(0, 0)
            k_out(0, 0)
            heads(0)
            with act.Fori(1, G - 1) as g:
                context_high(g - 1, HG - 1)
                heads(g)
            context_high(G - 2, HG - 1)
            heads(G - 1)
            context_high(G - 1, HG - 1)

            def x3_high(g):
                for i in range(GT):
                    bk_, u = t3_use(g, i)
                    act.wait_ge(filled[bk_], u + 1)
                    act.activation(cT_hi[:, :, i * S:(i + 1) * S], bank[bk_][:].rearrange("p (k s) -> p k s", k=KT),
                                   ACT.Copy).then_inc(x3_hi_ready, 1)

            def high(g, f):
                bk_, u = gu_use(("U", f), g)
                act.wait_ge(drained[bk_], 2 * (u + 1))
                if is_now(g, 0) and f == LATE_SLICE:
                    for b_ in range(NPB):
                        act.wait_ge(proj_drained[b_], PROJ_END)
                act.activation(f_hi[:, f, :], fused[:, f % 2, :], ACT.Copy).then_inc(f_hi_ready, 1)

            def gates(g):
                for f in range(FT):
                    bk_, u = gu_use(("G", f), g)
                    act.wait_ge(filled[bk_], u + 1)
                    act.activation(tanh_g[:, f % 2, :], bank[bk_][:], ACT.Tanh, scale=half_gate[:, f:f + 1])\
                        .then_inc(tanh_ready, 1)
                    if f >= 1:
                        high(g, f - 1)
                    if is_now(g, 0):
                        epilogue_slot(f, lambda k: slot(G, k))
                high(g, FT - 1)

            act.wait_ge(fuse_c_made, 3)
            gates(0)
            x3_high(1)
            with act.Fori(1, G - 1) as g:
                gates(g)
                x3_high(g + 1)
            gates(G - 1)

        @block.vector
        def _(dve):
            def norm_stats(n, i, tile):
                dve.bn_stats(bn[:, i, :], tile).then_inc(bn_done, 1)

            def norm_moments(n):
                for i in range(GT):
                    wait_apart(dve, bn_done, n * GT + i + 1)
                    dve.bn_aggr(mv[:, i, :], bn[:, i, :]).then_inc(var_ready, 1)

            def norm_apply(n, tile):
                dve.wait_ge(rstd_ready, n + 1)
                for i in range(GT):
                    dve.tensor_scalar(xn[:, i, :], tile(i), mv[:, i, 0:1], rstd[:, i:i + 1], ALU.subtract,
                                      ALU.mult).then_inc(xn_ready, 1)

            def norm(n, tile):
                for i in range(GT):
                    norm_stats(n, i, tile(i))
                norm_moments(n)
                norm_apply(n, tile)

            def x_low(name, i, g):
                b_, u = proj_use((name, i), g)
                dve.wait_ge(xT_hi_ready, GT * (g + (name == "N")) + i + 1)
                dve.tensor_tensor(xT_lo[:, :, i * S:(i + 1) * S], proj_bank[b_][:].rearrange("p (k s) -> p k s", k=KT),
                                  xT_hi[:, :, i * S:(i + 1) * S].bitcast(F32), ALU.subtract)\
                    .then_inc(proj_drained[b_], 2)

            def v_out(g, tiles=range(GT)):
                for i in tiles:
                    src = wait_proj(dve, ("V", i), g)
                    dve.tensor_tensor(v[:, i, :], src[:], bv_b[:], ALU.add).then_inc(proj_sem(("V", i), g), 2)

            def wo_out(g, tiles=range(GT)):
                for i in tiles:
                    src = wait_proj(dve, ("WO", i), g)
                    t = token_tile(g - 1, i)
                    dve.wait_ge(bo_added, (g - 1) * GT + i + 1)
                    dve.tensor_tensor(t, src[:], t, ALU.add).then_inc(proj_sem(("WO", i), g), 2)
                    b_, u = proj_use(("WO", i), g)
                    wait_apart(dve, proj_drained[b_], 2 * (u + 1))
                    if i < GT - 1 or is_now(g, G):
                        norm_stats(2 * g, i, t)

            def alibi_add(g, hg):
                m = g * HG + hg
                for i in range(GT):
                    dve.wait_ge(scores_filled, m * GT + i + 1)
                    dve.tensor_tensor(probs[:, i].rearrange("p j s -> p (j s)"), score_bank[i % NSB][:],
                                      alibi[:, 4 * hg:4 * hg + 4].rearrange("p j s -> p (j s)"), ALU.add)\
                        .then_inc(biased, 1)

            def normalize_context(g, hg):
                m = g * HG + hg
                dve.wait_ge(ctx_filled, m + 1)
                if not (is_now(g, 0) and hg == 0):
                    dve.wait_ge(ctx_lo, m)
                dve.reciprocal(ctxT[:], den_bank[:]).then_inc(recip_done, 1)
                dve.wait_ge(recip_done, m + 1)
                dve.tensor_tensor(ctxT[:], ctx_bank[:], ctxT[:], ALU.mult).then_inc(ctx_normed, 1)

            def masks(g):
                at = g - 1
                dve.tensor_copy(mask_cap[:], mask_u8[:, bass.ds(at * GT, GT), :]).then_inc(mask_step, 1)
                dve.wait_ge(mask_step, 1 + at)
                dve.tensor_reduce(valid[:], mask_cap[:], AX.X, ALU.max).then_inc(mask_ready, 1)
                wait_apart(dve, mask_ready, 2 * at + 1)
                dve.tensor_scalar(mask_cap[:], mask_cap[:], UNBOUNDED, -NEG, ALU.mult, ALU.add).then_inc(mask_ready, 1)

            def slot(g, k):
                for name, i in slot_items(g, k):
                    n = i % 2
                    at = (g - 1) * GT + i
                    if name == "XS":
                        src = wait_proj(dve, ("XS", i), g)
                        dve.wait_ge(mask_ready, 2 * g)
                        dve.scalar_tensor_tensor(x_sc[:, n, :], src[:, 0:S], X_SCALE, mask_cap[:, i, :], ALU.mult,
                                                 ALU.min).then_inc(proj_sem(("XS", i), g), 2)
                        b_, u = proj_use(("XS", i), g)
                        dve.wait_ge(proj_drained[b_], 2 * (u + 1))
                        dve.tensor_reduce(x_bias[:, n:n + 1], x_sc[:, n, :], AX.X, ALU.max, negate=True)\
                            .then_inc(xs_ready, 1)
                    if name == "RO":
                        dve.wait_ge(xs_exped, at + 1)
                        dve.reciprocal(x_rec[:, n:n + 1], x_den[:, n:n + 1]).then_inc(xs_weight, 1)
                        dve.wait_ge(xs_weight, 2 * at + 1)
                        dve.tensor_tensor(x_w[:, n:n + 1], x_rec[:, n:n + 1], valid[:, i:i + 1], ALU.mult)\
                            .then_inc(xs_weight, 1)
                        dve.wait_ge(xs_weight, 2 * at + 2)
                        src = wait_proj(dve, ("RO", i), g)
                        t = token_tile(g - 1, i)
                        dve.scalar_tensor_tensor(t, src[:], x_w[:, n:n + 1], t, ALU.mult, ALU.add)\
                            .then_inc(proj_sem(("RO", i), g), 2)

            def prepare_slab(g, n):
                at = (g - 1) * SLABS + n
                w, m, z = q_w[:, n % Q_BUFS, :], q_m[:, n % 2, :], q_z[:]
                dve.wait_ge(q_loaded[n % Q_BUFS], 16 * (n // Q_BUFS + 1) + (g - 1) * (16 * SLABS // Q_BUFS))
                if n > 0:
                    dve.wait_ge(q_prepared, 2 * at)
                if n > 1:
                    dve.wait_ge(q_rounded, at - 1)
                dve.tensor_scalar(m.bitcast(U32), w.bitcast(U32), EXPONENT_BITS, None, ALU.bitwise_and)\
                    .then_inc(q_step, 1)
                dve.tensor_scalar(z, w, TO_ONE, TO_RANGE_END, ALU.mult, ALU.mult).then_inc(q_step, 1)
                dve.wait_ge(q_step, 2 * at + 2)
                dve.tensor_scalar(m, m, MIN_NORMAL, ROUNDER, ALU.max, ALU.mult).then_inc(q_prepared, 1)
                dve.scalar_tensor_tensor(w, z, 0.0, w, ALU.mult, ALU.add).then_inc(q_prepared, 1)

            def prepares(g, slabs):
                if not is_now(g, 0):
                    for n in slabs:
                        prepare_slab(g, n)

            def heads(g):
                def next_tile(i):
                    return next_group_tile(g, i)

                for hg in range(HG):
                    alibi_add(g, hg)
                    if hg > 0:
                        normalize_context(g, hg - 1)
                    elif not is_now(g, 0):
                        norm_stats(2 * g, GT - 1, token_tile(g - 1, GT - 1))
                        norm_moments(2 * g)
                        norm_apply(2 * g, lambda i: token_tile(g - 1, i))
                    for k in (2 * hg, 2 * hg + 1):
                        slot(g, k)
                        prepares(g, slabs_at(g, k))
                        if k < GT:
                            if is_now(g, 0) and k == 0:
                                dve.wait_ge(x_rest_loaded, 16)
                            norm_stats(2 * g + 1, k, next_tile(k))
                        if k == GT - 1:
                            norm_moments(2 * g + 1)
                        if k == GT:
                            if not is_now(g, 0):
                                wait_proj(dve, ("T2", GT - 1), g)
                            norm_apply(2 * g + 1, next_tile)
                        for name, i in after_slot(k):
                            x_low(name, i, g)

            for i in range(GT):
                dve.wait_ge(x_first_loaded[i], 16)
                norm_stats(0, i, token_tile(0, i))
            norm_moments(0)
            norm_apply(0, lambda i: token_tile(0, i))

            def weight_low(n, m):
                dve.wait_ge(w_hi_made, n + 1)
                hi, lo = (w_hi[:, m], w_lo[:, m]) if m < 3 else (wo_hi, wo_lo)
                dve.tensor_tensor(lo.rearrange("p k n -> p (k n)"), raw[m],
                                  hi.rearrange("p k n -> p (k n)").bitcast(F32), ALU.subtract)\
                    .then_inc(w_lo_made, 1)

            weight_low(0, 2)
            for i in range(GT):
                x_low("T1", i, 0)
            weight_low(1, 0)
            dve.wait_ge(params_loaded, 16 * 8)
            v_out(0, (0,))
            weight_low(2, 1)
            v_out(0, (1, 2, 3))
            weight_low(3, 3)
            dve.wait_ge(rel_made, 1)
            for h in range(H):
                ins = dve.tensor_scalar(alibi[:, h, :], rel[:], slope_b[:, h:h + 1], None, ALU.mult)
            ins.then_inc(alibi_made, 1)
            dve.tensor_scalar(half_gate[:], gate_c[:], 0.5, None, ALU.mult).then_inc(fuse_c_made, 1)
            dve.tensor_tensor(fuse_c[:], gate_c[:], up_c[:], ALU.mult).then_inc(fuse_c_made, 1)
            dve.wait_ge(fuse_c_made, 2)
            dve.tensor_scalar(fuse_c[:], fuse_c[:], 0.5, None, ALU.mult).then_inc(fuse_c_made, 1)
            dve.wait_ge(alibi_made, 1)
            heads(0)
            def iteration(g):
                normalize_context(g - 1, HG - 1)
                v_out(g, (0, 1))
                prepares(g, (0,))
                v_out(g, (2,))
                prepares(g, (1,))
                v_out(g, (3,))
                masks(g)
                prepares(g, (2,))
                wo_out(g, (0,))
                prepares(g, (3,))
                wo_out(g, (1, 2, 3))
                heads(g)

            with dve.Fori(1, G - 1) as g:
                iteration(g)
            iteration(G - 1)
            normalize_context(G - 1, HG - 1)
            prepares(G - 1, LATE_SLABS)
            masks(G)

            def x3_low(g):
                for i in range(GT):
                    bk_, u = t3_use(g, i)
                    dve.wait_ge(x3_hi_ready, (g - 1) * GT + i + 1)
                    dve.tensor_tensor(cT_lo[:, :, i * S:(i + 1) * S], bank[bk_][:].rearrange("p (k s) -> p k s", k=KT),
                                      cT_hi[:, :, i * S:(i + 1) * S].bitcast(F32), ALU.subtract)\
                        .then_inc(drained[bk_], 2)

            def fuse(g, slices=range(FT)):
                for f in slices:
                    at = g * FT + f
                    bg, ug = gu_use(("G", f), g)
                    bu, uu = gu_use(("U", f), g)
                    dve.wait_ge(tanh_ready, at + 1)
                    dve.scalar_tensor_tensor(silu2[:, f % 2, :], tanh_g[:, f % 2, :], 1.0, bank[bg][:], ALU.add, ALU.mult)\
                        .then_inc(drained[bg], 2)
                    dve.wait_ge(drained[bg], 2 * (ug + 1))
                    dve.wait_ge(filled[bu], uu + 1)
                    if f >= 2:
                        dve.wait_ge(f_lo_ready, at - 1)
                    dve.scalar_tensor_tensor(fused[:, f % 2, :], bank[bu][:], fuse_c[:, f:f + 1], silu2[:, f % 2, :],
                                             ALU.mult, ALU.mult).then_inc(drained[bu], 2)
                    if is_now(g, 0):
                        if f == BEFORE_WO:
                            norm_apply(2 * G, lambda i: token_tile(G - 1, i))
                        epilogue_slot(f, lambda k: slot(G, k))
                        if f == NORM_AT - 1:
                            for i in range(GT):
                                norm_stats(2 * G + 1, i, token_tile(1, i))
                            norm_moments(2 * G + 1)
                        if f == NORM_AT:
                            wait_proj(dve, ("T2", GT - 1), G)
                            norm_apply(2 * G + 1, lambda i: token_tile(1, i))

            def y_out(g):
                dve.wait_ge(down_c_loaded, 16)
                for i in range(GT):
                    bk_, u = gu_use(("D", i), g)
                    at = g * GT + i
                    dve.wait_ge(filled[bk_], u + 1)
                    if i >= 2:
                        dve.wait_ge(y_stored[i % 2], 16 * (i // 2) + g * 32)
                    elif not is_now(g, 0):
                        dve.wait_ge(y_stored[i % 2], g * 32)
                    dve.tensor_tensor(y_sb[:, i % 2, :], bank[bk_][:], down_c[:], ALU.mult).then_inc(drained[bk_], 2)
                    dve.wait_ge(drained[bk_], 2 * (u + 1))
                    dve.tensor_tensor(y_sb[:, i % 2, :], y_sb[:, i % 2, :], token_tile(g, i), ALU.add)\
                        .then_inc(y_ready, 1)

            fuse(0, range(BEFORE_WO))
            wo_out(G)
            norm_moments(2 * G)
            fuse(0, range(BEFORE_WO, FT))
            x3_low(1)
            y_out(0)
            with dve.Fori(1, G - 1) as g:
                norm(g + 2 * G + 1, lambda i: token_tile(g + 1, i))
                fuse(g)
                x3_low(g + 1)
                y_out(g)
            fuse(G - 1)
            y_out(G - 1)

        @block.tensor
        def _(pe):
            def take(item, g):
                b_, u = proj_use(item, g)
                if not (is_now(g, 0) and u == 0):
                    pe.wait_ge(proj_drained[b_], 2 * u)
                return proj_bank[b_], proj_filled[b_]

            def transposes(dst, n, i):
                pe.wait_ge(xn_ready, n * GT + i + 1)
                for k in range(KT):
                    ins = pe.transpose(dst[:, k * S:(k + 1) * S], xn[:, i, k * P:(k + 1) * P], identity[:])
                return ins

            def t1(name, i, g, n):
                dst, done = take((name, i), g)
                transposes(dst, n, i).then_inc(done, 1)

            def products(dst, pairs):
                for n, (stationary, moving) in enumerate(pairs):
                    ins = pe.matmul(dst, stationary, moving, start=(n == 0), stop=(n == len(pairs) - 1))
                return ins

            def v_proj(g):
                for i in range(GT):
                    if is_now(g, 0):
                        b_, u = proj_use(("T1", i), 0)
                        pe.wait_ge(proj_drained[b_], 2 * (u + 1))
                    dst, done = take(("V", i), g)
                    t = slice(i * S, (i + 1) * S)
                    products(dst[:], [p for k in range(KT) for p in (
                        (xT_hi[:, k, t], w_hi[:, 2, k]), (xT_hi[:, k, t], w_lo[:, 2, k]),
                        (xT_lo[:, k, t], w_hi[:, 2, k]))]).then_inc(done, 1)

            def wo_proj(g):
                pe.wait_ge(ctx_lo, g * HG)
                for i in range(GT):
                    dst, done = take(("WO", i), g)
                    t = slice(i * S, (i + 1) * S)
                    products(dst[:], [p for k in range(KT) for p in (
                        (cT_hi[:, k, t], wo_hi[:, k]), (cT_hi[:, k, t], wo_lo[:, k]),
                        (cT_lo[:, k, t], wo_hi[:, k]))]).then_inc(done, 1)

            def qk_proj(g, name, hg):
                m = "QK".index(name)
                dst, done = take((name, hg), g)
                n = slice(hg % HG * P, (hg % HG + 1) * P)
                products(dst[:], [p for k in range(KT) for p in (
                    (w_hi[:, m, k, n], xT_hi[:, k]), (w_hi[:, m, k, n], xT_lo[:, k]),
                    (w_lo[:, m, k, n], xT_hi[:, k]))]).then_inc(done, 1)

            def scores(g, hg):
                m = g * HG + hg
                if hg == 0 and not is_now(g, 0):
                    for b_ in range(NPB):
                        pe.wait_ge(proj_drained[b_], 2 * uses_before(b_, g))
                else:
                    for name in ("Q", "K"):
                        b_, u = proj_use((name, hg), g)
                        pe.wait_ge(proj_drained[b_], 2 * (u + 1))
                for i in range(GT):
                    t = slice(i * S, (i + 1) * S)
                    if not (is_now(g, 0) and hg == 0 and i < NSB):
                        pe.wait_ge(biased, m * GT - NSB + i + 1)
                    pe.matmul(score_bank[i % NSB][:], kT[:, t], qbd[:, :, t], start=True, stop=True)\
                        .then_inc(scores_filled, 1)

            def context(g, hg):
                m = g * HG + hg
                if not (is_now(g, 0) and hg == 0):
                    pe.wait_ge(ctx_normed, m)
                if hg == 0:
                    b_, u = proj_use(("V", GT - 1), g)
                    pe.wait_ge(proj_drained[b_], 2 * (u + 1))
                    b_, u = proj_use(("V", GT - 2), g)
                    pe.wait_ge(proj_drained[b_], 2 * (u + 1))
                for i in range(GT):
                    t = slice(i * S, (i + 1) * S)
                    pe.wait_ge(masked, m * GT + i + 1)
                    for j in range(4):
                        rows = slice(HD * j, HD * (j + 1))
                        col = hg * P + HD * j
                        pe.matmul(ctx_bank[rows, t], v[:, i, col:col + HD], probs[:, i, j, :], start=True, stop=True)
                    for j in range(4):
                        rows = slice(HD * j, HD * (j + 1))
                        ins = pe.matmul(den_bank[rows, t], ones[:], probs[:, i, j, :], start=True, stop=True)
                ins.then_inc(ctx_filled, 1)

            def slot(g, k):
                for name, i in slot_items(g, k):
                    n = i % 2
                    dst, done = take((name, i), g)
                    if name == "T2":
                        transposes(dst, 2 * g, i).then_inc(done, 1)
                    if name == "XS":
                        b_, u = proj_use(("T2", i), g)
                        pe.wait_ge(proj_drained[b_], 2 * (u + 1))
                        pe.wait_ge(memT_loaded[n], 16 * (i // 2 + 1) + (g - 1) * 32)
                        products(dst[:, 0:S], [(x2T[:, k_, :], memT_sb[:, n, k_, :]) for k_ in range(KT)])\
                            .then_inc(done, 1)
                    if name == "PT":
                        pe.wait_ge(xs_exped, (g - 1) * GT + i + 1)
                        pe.transpose(dst[:, 0:S], x_sc[:, n, :], identity[:]).then_inc(done, 1)
                    if name == "RO":
                        b_, u = proj_use(("PT", i), g)
                        pe.wait_ge(proj_drained[b_], 2 * (u + 1))
                        pe.wait_ge(mem_loaded[n], 16 * (i // 2 + 1) + (g - 1) * 32)
                        pe.matmul(dst[:], x_pT[:, n, :], mem_sb[:, n, :], start=True, stop=True).then_inc(done, 1)

            def heads(g):
                for hg in range(HG):
                    scores(g, hg)
                    for k in (2 * hg, 2 * hg + 1):
                        for name, i in before_slot(g, k):
                            if i == HG and name == "Q":
                                for n in range(GT):
                                    b_, u = proj_use(("N", n), g)
                                    pe.wait_ge(proj_drained[b_], 2 * (u + 1))
                            qk_proj(g, name, i)
                        slot(g, k)
                        for name, i in after_slot(k):
                            t1(name, i, g, 2 * g + 1)
                    context(g, hg)

            pe.wait_ge(identity_made, 1)
            for i in range(GT):
                t1("T1", i, 0, 0)
            pe.wait_ge(w_lo_made, 1)
            v_proj(0)
            pe.wait_ge(w_lo_made, 3)
            for name in "QK":
                qk_proj(0, name, 0)
            heads(0)
            with pe.Fori(1, G - 1) as g:
                v_proj(g)
                wo_proj(g)
                heads(g)
            v_proj(G - 1)
            wo_proj(G - 1)
            heads(G - 1)

            def ffn_take(bk_, u):
                if not (isinstance(u, int) and u == 0):
                    pe.wait_ge(drained[bk_], 2 * u)
                return bank[bk_]

            def t3(g):
                for i in range(GT):
                    bk_, u = t3_use(g, i)
                    dst = ffn_take(bk_, u)
                    transposes(dst, g + 2 * G, i).then_inc(filled[bk_], 1)

            def gate_up(g, slices=range(FT)):
                for i in range(GT if not is_now(g, 0) else 0):
                    bk_, u = t3_use(g, i)
                    pe.wait_ge(drained[bk_], 2 * (u + 1))
                if is_now(g, 0):
                    for i in range(GT):
                        b_, u = proj_use(("N", i), G - 1)
                        pe.wait_ge(proj_drained[b_], 2 * (u + 1))
                for f in slices:
                    pe.wait_ge(gu_loaded[f], 16)
                    if is_now(g, 0) and f == 0:
                        pe.wait_ge(biased, G * HG * GT)
                    if is_now(g, 0) and f == 1:
                        pe.wait_ge(ctx_normed, G * HG)
                    for w, name in ((0, "G"), (1, "U")):
                        bk_, u = gu_use((name, f), g)
                        dst = ffn_take(bk_, u)
                        products(dst[:], [(gu_w[:, f, w, k], part[:, k]) for k in range(KT) for part in x3[g if is_now(g, 0) else 1]])\
                            .then_inc(filled[bk_], 1)
                    if is_now(g, 0):
                        epilogue_slot(f, lambda k: slot(G, k))

            def down(g):
                for i in range(GT):
                    bk_, u = gu_use(("D", i), g)
                    dst = ffn_take(bk_, u)
                    t = slice(i * S, (i + 1) * S)
                    for f in range(FT):
                        if i == 0:
                            pe.wait_ge(f_lo_ready, g * FT + f + 1)
                        if is_now(g, 0) and i == 0 and f in (0, FD):
                            pe.wait_ge(down_loaded if f == 0 else down_late_loaded, 16)
                        for n, part in enumerate((f_hi, f_lo)):
                            ins = pe.matmul(dst[:], part[:, f, t], down_q[:, f], start=(f + n == 0),
                                            stop=(f + n == FT))
                    ins.then_inc(filled[bk_], 1)

            gate_up(0, range(BEFORE_WO))
            wo_proj(G)
            gate_up(0, range(BEFORE_WO, FT))
            for b_ in range(NPB):
                pe.wait_ge(proj_drained[b_], PROJ_END)
            t3(1)
            down(0)
            with pe.Fori(1, G - 1) as g:
                gate_up(g)
                t3(g + 1)
                down(g)
            gate_up(G - 1)
            down(G - 1)


def kernel(**inputs):
    import numpy as np
    import concourse.bacc as bacc
    from concourse.bass_utils import run_bass_kernel_spmd

    a = {k: np.asarray(v) for k, v in inputs.items()}

    def per_partition(vector):
        return np.ascontiguousarray(vector.reshape(-1, P).T)

    arrays = {
        "x": a["x"],
        "memT": np.ascontiguousarray(a["ctx_2048"].transpose(0, 2, 1)),
        "mem": a["ctx_2048"],
        "mask": np.ascontiguousarray(a["mask_BxS2_bk0"]).reshape(B * S),
        "wT": np.stack([a["L0_attn_W" + n].T for n in "qkvo"]),
        "bq": per_partition(a["L0_attn_bq"]), "bk": per_partition(a["L0_attn_bk"]),
        "bv": a["L0_attn_bv"], "bo": a["L0_attn_bo"], "slopes": a["L0_attn_alibi_slopes"],
        "gate_w": a["L0_ffn_gate_w"], "up_w": a["L0_ffn_up_w"], "down_w": a["L0_ffn_down_w"],
        "gate_s": per_partition(a["L0_ffn_gate_scale"]), "up_s": per_partition(a["L0_ffn_up_scale"]),
        "down_s": a["L0_ffn_down_scale"],
    }
    nc = bacc.Bacc("TRN2", target_bir_lowering=False, num_devices=1)
    arrays = {f"in_{k}": np.ascontiguousarray(v) for k, v in arrays.items()}
    args = [nc.dram_tensor(k, v.shape, mybir.dt.from_np(v.dtype), kind="ExternalInput").ap()
            for k, v in arrays.items()]
    out = nc.dram_tensor("out", (B, S, D), F32, kind="ExternalOutput").ap()
    build(nc, *args, out)
    r = run_bass_kernel_spmd(nc, [arrays], core_ids=[0])
    return r.results[0]["out"]
```
